# Optimizing a Trainium2 kernel written in Bass

```python
import numpy as np
import jax
import jax.numpy as jnp

def _softmax(x, axis=-1):
    return jax.nn.softmax(x, axis=axis)

def _gelu(x):
    return jax.nn.gelu(x, approximate=True)

def _silu(x):
    return jax.nn.silu(x)

def _sigmoid(x):
    return jax.nn.sigmoid(x)

def _layernorm(x, axis=-1, eps=1e-05):
    m = jnp.mean(x, axis=axis, keepdims=True)
    v = jnp.var(x, axis=axis, keepdims=True)
    return (x - m) / jnp.sqrt(v + eps)

def _scatter_add(tgt, idx, src, axis=0):
    return tgt.at[idx].add(src)

def _segment_sum(src, seg, n):
    return jax.ops.segment_sum(src, seg, n)
kernel_name = 'mk_adaln_ffn_d2_seqx_r4_fe49bf'

def setup_inputs(seed: int=0):
    np.random.seed(seed)
    _w = jnp.asarray

    def _rec_inputs():
        import jax
        import jax.numpy as jnp
        _rk = jax.random.key(seed)
        x = -0.000125 + 0.9999 * jax.random.normal(jax.random.fold_in(_rk, 1), (32, 64, 1024), jnp.float32)
        _lenS = 64 - jax.random.randint(jax.random.fold_in(_rk, 7), (32,), 0, max(1, 64 // 4) + 1, jnp.int32)
        _lenS2 = 64 - jax.random.randint(jax.random.fold_in(_rk, 8), (32,), 0, max(1, 64 // 4) + 1, jnp.int32)
        cond_128 = 0.0061147 + 1.02565 * jax.random.normal(jax.random.fold_in(_rk, 11), (32, 128), jnp.float32)
        fside_S_0 = -0.022604 + 0.987366 * jax.random.normal(jax.random.fold_in(_rk, 12), (64,), jnp.float32)
        return (x, cond_128, fside_S_0)
    x, cond_128, fside_S_0 = _rec_inputs()

    def _L0_cond_setup():
        import jax, jax.numpy as jnp
        import numpy as np
        K = 8
        T = 1.0
        D_EMBD = 128
        IN_C = 64
        OUT_C = 64
        BS = 32
        H = 1024
        HID = 128
        key = jax.random.key(seed)
        ks = jax.random.split(key, 10)
        s = lambda fan_in: 1.0 / np.sqrt(fan_in)
        return {'x': jax.random.normal(ks[0], (BS, IN_C, H), dtype=jnp.float32), 'embedding': jax.random.normal(ks[1], (BS, D_EMBD), dtype=jnp.float32), 'W0': jax.random.normal(ks[2], (D_EMBD, HID), dtype=jnp.float32) * s(D_EMBD), 'b0': jnp.zeros((HID,), dtype=jnp.float32), 'W1': jax.random.normal(ks[3], (HID, HID), dtype=jnp.float32) * s(HID), 'b1': jnp.zeros((HID,), dtype=jnp.float32), 'W2': jax.random.normal(ks[4], (HID, K), dtype=jnp.float32) * s(HID), 'b2': jnp.zeros((K,), dtype=jnp.float32), 'weight': jax.random.normal(ks[5], (K, OUT_C, IN_C, 1), dtype=jnp.float32) * s(IN_C), 'bias_k': jax.random.normal(ks[6], (K, OUT_C), dtype=jnp.float32) * 0.1}
    _L0_cond_all = _L0_cond_setup()
    _L0_cond_in = {k: v for k, v in _L0_cond_all.items() if k in ('W0', 'b0', 'W1', 'b1', 'W2', 'b2', 'weight', 'bias_k')}
    del _L0_cond_all

    def _L0_ffn_setup():
        import jax, jax.numpy as jnp
        import numpy as np
        TOP_K = 2
        key = jax.random.key(seed)
        k1, k2, k3 = jax.random.split(key, 3)
        B, S, H, O, E = (2048, 1, 1024, 1024, 8)
        x = jax.random.normal(k1, (B, S, H), dtype=jnp.float32)
        gate_w = jax.random.normal(k2, (H, E), dtype=jnp.float32) * 0.02
        expert_w = jax.random.normal(k3, (E, H, O), dtype=jnp.float32) * 0.02
        return {'x': x, 'gate_w': gate_w, 'expert_w': expert_w}
    _L0_ffn_all = _L0_ffn_setup()
    _L0_ffn_in = {k: v for k, v in _L0_ffn_all.items() if k in ('gate_w', 'expert_w')}
    del _L0_ffn_all

    def _L1_cond_setup():
        import jax, jax.numpy as jnp
        import numpy as np
        from jax import lax
        N, C_IN, L = (32, 64, 1024)
        C_OUT, K, GROUPS = (64, 9, 4)
        C_DIM, PAD, STRIDE = (128, 4, 1)
        key = jax.random.key(seed)
        k1, k2, k3, k4, k5 = jax.random.split(key, 5)
        x = jax.random.normal(k1, (N, C_IN, L), dtype=jnp.float32)
        c = jax.random.normal(k2, (N, C_DIM), dtype=jnp.float32)
        weight = jax.random.normal(k3, (C_OUT, C_IN // GROUPS, K), dtype=jnp.float32)
        c_weight = jax.random.normal(k4, (C_OUT, C_DIM), dtype=jnp.float32)
        bias = jax.random.normal(k5, (C_OUT,), dtype=jnp.float32)
        return {'x': x, 'c': c, 'weight': weight, 'c_weight': c_weight, 'bias': bias}
    _L1_cond_all = _L1_cond_setup()
    _L1_cond_in = {k: v for k, v in _L1_cond_all.items() if k in ('weight', 'c_weight')}
    del _L1_cond_all

    def _L1_ffn_setup():
        import jax, jax.numpy as jnp
        import numpy as np
        B, S, IN, OUT = (4, 512, 1024, 1024)
        E, K, R = (8, 2, 16)
        CAP_FACTOR = 3.0
        ALPHA = 1.0 / R
        LN_EPS = 1e-05
        key = jax.random.key(seed)
        ks = jax.random.split(key, 6)
        return {'x': jax.random.normal(ks[0], (B, S, IN), dtype=jnp.float32), 'weight': jax.random.normal(ks[1], (OUT, IN), dtype=jnp.float32) * 0.02, 'lora_A': jax.random.normal(ks[2], (E, IN, R), dtype=jnp.float32) / np.sqrt(R), 'lora_B': jax.random.normal(ks[3], (E, R, OUT), dtype=jnp.float32) * 0.02, 'gw1': jax.random.normal(ks[4], (4 * E, IN), dtype=jnp.float32) * 0.02, 'gb1': jnp.zeros((4 * E,), dtype=jnp.float32), 'ln_gamma': jnp.ones((4 * E,), dtype=jnp.float32), 'ln_beta': jnp.zeros((4 * E,), dtype=jnp.float32), 'gw2': jax.random.normal(ks[5], (E, 4 * E), dtype=jnp.float32) * 0.02, 'gb2': jnp.zeros((E,), dtype=jnp.float32)}
    _L1_ffn_all = _L1_ffn_setup()
    _L1_ffn_in = {k: v for k, v in _L1_ffn_all.items() if k in ('weight', 'lora_A', 'lora_B', 'gw1', 'gb1', 'ln_gamma', 'ln_beta', 'gw2', 'gb2')}
    del _L1_ffn_all
    return {'x': x, 'cond_128': cond_128, 'fside_S_0': fside_S_0, 'L0_cond_W0': _L0_cond_in['W0'], 'L0_cond_b0': _L0_cond_in['b0'], 'L0_cond_W1': _L0_cond_in['W1'], 'L0_cond_b1': _L0_cond_in['b1'], 'L0_cond_W2': _L0_cond_in['W2'], 'L0_cond_b2': _L0_cond_in['b2'], 'L0_cond_weight': _L0_cond_in['weight'], 'L0_cond_bias_k': _L0_cond_in['bias_k'], 'L0_ffn_gate_w': _L0_ffn_in['gate_w'], 'L0_ffn_expert_w': _L0_ffn_in['expert_w'], 'L1_cond_weight': _L1_cond_in['weight'], 'L1_cond_c_weight': _L1_cond_in['c_weight'], 'L1_ffn_weight': _L1_ffn_in['weight'], 'L1_ffn_lora_A': _L1_ffn_in['lora_A'], 'L1_ffn_lora_B': _L1_ffn_in['lora_B'], 'L1_ffn_gw1': _L1_ffn_in['gw1'], 'L1_ffn_gb1': _L1_ffn_in['gb1'], 'L1_ffn_ln_gamma': _L1_ffn_in['ln_gamma'], 'L1_ffn_ln_beta': _L1_ffn_in['ln_beta'], 'L1_ffn_gw2': _L1_ffn_in['gw2'], 'L1_ffn_gb2': _L1_ffn_in['gb2']}

def reference(x, cond_128, fside_S_0, L0_cond_W0, L0_cond_b0, L0_cond_W1, L0_cond_b1, L0_cond_W2, L0_cond_b2, L0_cond_weight, L0_cond_bias_k, L0_ffn_gate_w, L0_ffn_expert_w, L1_cond_weight, L1_cond_c_weight, L1_ffn_weight, L1_ffn_lora_A, L1_ffn_lora_B, L1_ffn_gw1, L1_ffn_gb1, L1_ffn_ln_gamma, L1_ffn_ln_beta, L1_ffn_gw2, L1_ffn_gb2):
    import jax
    import jax.numpy as jnp

    def _L0_cond_ref(x, embedding, W0, b0, W1, b1, W2, b2, weight, bias_k):
        import jax, jax.numpy as jnp
        import numpy as np
        K = 8
        T = 1.0
        D_EMBD = 128
        IN_C = 64
        OUT_C = 64
        BS = 32
        H = 1024
        HID = 128
        h = jax.nn.gelu(embedding @ W0 + b0, approximate=False)
        h = jax.nn.gelu(h @ W1 + b1, approximate=False)
        att = jax.nn.softmax((h @ W2 + b2) / T, axis=-1)
        agg_w = jnp.einsum('bk,koi->boi', att, weight[..., 0])
        agg_b = att @ bias_k
        out = jnp.einsum('boi,bih->boh', agg_w, x) + agg_b[:, :, None]
        return out

    def _L0_ffn_ref(x, gate_w, expert_w):
        import jax, jax.numpy as jnp
        import numpy as np
        TOP_K = 2
        E = gate_w.shape[-1]
        logits = jnp.einsum('bsh,he->bse', x, gate_w)
        topv, topi = jax.lax.top_k(logits, TOP_K)
        w = jax.nn.softmax(topv, axis=-1)
        onehot = jax.nn.one_hot(topi, E, dtype=x.dtype)
        w_e = jnp.einsum('bske,bsk->bse', onehot, w)
        out = jnp.einsum('bsh,eho,bse->bso', x, expert_w, w_e)
        return out

    def _L1_cond_ref(x, c, weight, c_weight, bias):
        import jax, jax.numpy as jnp
        import numpy as np
        from jax import lax
        N, C_IN, L = (32, 64, 1024)
        C_OUT, K, GROUPS = (64, 9, 4)
        C_DIM, PAD, STRIDE = (128, 4, 1)
        out = lax.conv_general_dilated(x, weight, window_strides=(STRIDE,), padding=[(PAD, PAD)], dimension_numbers=('NCH', 'OIH', 'NCH'), feature_group_count=GROUPS)
        ctx = jnp.einsum('nd,od->no', c, c_weight)
        out = out + ctx[:, :, None] + bias[None, :, None]
        return out

    def _L1_ffn_ref(x, weight, lora_A, lora_B, gw1, gb1, ln_gamma, ln_beta, gw2, gb2):
        import jax, jax.numpy as jnp
        import numpy as np
        B, S, IN, OUT = (4, 512, 1024, 1024)
        E, K, R = (8, 2, 16)
        CAP_FACTOR = 3.0
        ALPHA = 1.0 / R
        LN_EPS = 1e-05
        orig_shape = x.shape
        xf = x.reshape(-1, orig_shape[-1])
        N = xf.shape[0]
        capacity = int(CAP_FACTOR * N / E)
        h = xf @ gw1.T + gb1
        mu = jnp.mean(h, axis=-1, keepdims=True)
        var = jnp.mean((h - mu) ** 2, axis=-1, keepdims=True)
        h = (h - mu) * jax.lax.rsqrt(var + LN_EPS) * ln_gamma + ln_beta
        h = jax.nn.relu(h)
        gates = h @ gw2.T + gb2
        top_v, top_i = jax.lax.top_k(gates, K)
        top_g = jax.nn.softmax(top_v, axis=-1)
        onehot = (top_i[..., None] == jnp.arange(E)).astype(xf.dtype)
        counts = onehot.sum(axis=0)
        allowed = (counts <= capacity).astype(xf.dtype)
        w = jnp.einsum('nke,nk,ke->ne', onehot, top_g, allowed)
        main = xf @ weight.T
        tmp = jnp.einsum('ni,eir->enr', xf, lora_A)
        tmp = tmp * w.T[:, :, None]
        lora = jnp.einsum('enr,ero->no', tmp, lora_B) * ALPHA
        out = main + lora
        return out.reshape(*orig_shape[:-1], weight.shape[0])
    x = x + _L0_ffn_ref(_L0_cond_ref(x, cond_128, L0_cond_W0, L0_cond_b0, L0_cond_W1, L0_cond_b1, L0_cond_W2, L0_cond_b2, L0_cond_weight, L0_cond_bias_k), L0_ffn_gate_w, L0_ffn_expert_w)
    x = x + _L1_ffn_ref(_L1_cond_ref(x, cond_128, L1_cond_weight, L1_cond_c_weight, fside_S_0), L1_ffn_weight, L1_ffn_lora_A, L1_ffn_lora_B, L1_ffn_gw1, L1_ffn_gb1, L1_ffn_ln_gamma, L1_ffn_ln_beta, L1_ffn_gw2, L1_ffn_gb2)
    return x

_drawn_inputs = setup_inputs


def setup_inputs(seed=0):
    import zlib

    import numpy as np

    out = dict(_drawn_inputs(seed))
    spreads = {'L0_cond_b0': (0.0, 0.353),
     'L0_cond_b1': (0.0, 0.1),
     'L0_cond_b2': (0.0, 0.1),
     'L1_ffn_gb1': (0.0, 0.8),
     'L1_ffn_ln_gamma': (1.0, 0.6),
     'L1_ffn_ln_beta': (0.0, 0.647),
     'L1_ffn_gb2': (0.0, 0.1)}
    factors = {'L1_ffn_gw1': 2.678}
    for name, (base, spread) in spreads.items():
        noise = np.random.default_rng([zlib.crc32(name.encode()), seed]).standard_normal(out[name].shape)
        drawn = base * np.exp(spread * noise) if base else spread * noise
        out[name] = jnp.asarray(drawn.astype(out[name].dtype))
    for name, factor in factors.items():
        out[name] = (out[name] * factor).astype(out[name].dtype)
    return out
```

```python
from contextlib import ExitStack

import numpy as np

import concourse.bass as bass
from concourse import mybir

ALU = mybir.AluOpType
ACT = mybir.ActivationFunctionType
AX = mybir.AxisListType
F32 = mybir.dt.float32
I32 = mybir.dt.int32
U32 = mybir.dt.uint32

P = 128
B, CH, H = 32, 64, 1024
N = B * CH
NT = N // P
E = 8
K8 = 8
SLOTS = 2 * NT + E - 1
HC = H // P
HALF = H // 2
R = 16
HG = 4 * E
TAPS, PAD = 9, 4
PAIRS = (TAPS + 1) // 2
MW = H // 2 + 2 * (PAD // 2)
CAPACITY = int(3.0 * N / E)
ALPHA = 1.0 / R
LN_EPS = 1e-5
CREDIT, DMA_CREDIT = 1, 16
G1W = E * R + HG


def columns(widths):
    at, out = 0, {}
    for name, w in widths:
        out[name] = (at, at + w)
        at += w
    return out, at


CA, CA_W = columns([("emb", B), ("w0", P), ("w1", P), ("w2", K8), ("b0", 1), ("b1", 1), ("b2", K8),
                    ("gate", HC * E), ("kern", K8 * CH), ("kbias", K8), ("ident", P), ("tri", P),
                    ("ones", P), ("iota", E), ("thr", NT - 1), ("cw", CH), ("fside", CH)])
CB, CB_W = columns([("gb1", HG), ("gamma", HG), ("beta", HG), ("gb2", E), ("gw2", E * HG)])


class Chain:

    def __init__(self, eng, sem, base=0):
        self.eng, self.sem, self.base, self.n = eng, sem, base, 0

    def add(self, ins):
        ins.then_inc(self.sem, 1)
        self.n += 1
        return self.n

    def wait(self, n=None):
        self.eng.wait_ge(self.sem, self.base + (self.n if n is None else n))

    def link(self, ins):
        self.add(ins)
        self.wait()


def build(nc, x, x_t, consts_a, consts_b, tok_ids, zeros, expert_w, conv_w, down_w, main_w, lora_b, out):
    ctx = ExitStack()
    with ctx:
        def sb(name, shape, dt=F32):
            return ctx.enter_context(nc.sbuf_tensor(name, shape, dt))

        def sem(name):
            return ctx.enter_context(nc.semaphore(name))

        def dram(name, shape, dt=F32):
            return nc.dram_tensor(name, shape, dt, kind="Internal").ap()

        c0_d = dram("c0_scratch", [N, H])
        list_d = dram("list_scratch", [E * N, 1], I32)
        y_d = dram("y_scratch", [(SLOTS + 1) * P, H])

        bank = [ctx.enter_context(nc.psum_tensor(f"bank{i}", [P, 512], F32)) for i in range(8)]

        ca = sb("ca", [P, CA_W])
        cb = sb("cb", [P, CB_W])
        toks = sb("toks", [P, NT], I32)
        conv_sb = sb("conv_sb", [P, PAIRS, P])
        down_sb = sb("down_sb", [P, HC, G1W])
        main_sb = sb("main_sb", [P, HC, H])
        lora_sb = sb("lora_sb", [P, H])

        def c(name, rows=P):
            a, b = CA[name]
            return ca[0:rows, a:b]

        def d(name):
            a, b = CB[name]
            return cb[:, a:b]

        big = sb("big", [P, 2 * HC * H])
        w_sb = big[:, :].rearrange("p (b c n) -> p b c n", b=2, c=HC)
        res = big[:, :].rearrange("p (t n) -> p t n", t=NT)
        work = sb("work", [P, 9 * H])

        def row(i, n=1):
            return work[:, i * H:(i + n) * H]

        x_sb = [row(0), row(1)]
        xt_sb = [row(2), row(3)]
        c0_sb = [row(4), row(5)]
        xg = row(6)
        lhs = row(7).rearrange("p (c m) -> p c m", c=HC)
        yo = row(8)
        yg = [row(0, 2).rearrange("p (k n) -> p k n", k=2),
              row(2, 2).rearrange("p (k n) -> p k n", k=2)]
        xr = [row(4), row(5)]
        x1p = [sb(f"x1p{j}", [P, 2, MW]) for j in range(2)]
        c1 = [row(6).rearrange("p (c m) -> p c m", c=HC),
              row(7).rearrange("p (c m) -> p c m", c=HC)]
        down_all = sb("down_all", [P, NT, G1W])
        ctxb = sb("ctxb", [P, B, CH])

        h0 = sb("h0", [P, B])
        h1 = sb("h1", [P, B])
        at_l = sb("at_l", [B, K8])
        at_m = sb("at_m", [B, 1])
        at_n = sb("at_n", [B, 1])
        at_e = sb("at_e", [B, K8])
        at_s = sb("at_s", [B, 1])
        at_r = sb("at_r", [B, 1])
        att = sb("att", [B, K8])
        attx = sb("attx", [B, B, K8])
        attp = sb("attp", [P, NT * K8])
        gsum = sb("gsum", [P, E])
        aggb = sb("aggb", [P, NT])
        aggb_t = sb("aggb_t", [P, NT, K8])
        agg = [sb(f"agg{j}", [P, CH]) for j in range(2)]
        bd = [sb(f"bd{j}", [P, P]) for j in range(2)]
        g_sb = sb("g_sb", [P, 2 * E])
        lg = sb("lg", [P, 2, E])
        mx = sb("mx", [P, 2, 8])
        ix = sb("ix", [P, 2, 8], U32)
        mx_all = sb("mx_all", [P, NT, 2])
        ixf = sb("ixf", [P, 4])
        oh = sb("oh", [P, 2, 2, E])
        msk = sb("msk", [P, 2, E])
        pre = sb("pre", [P, 2, E])
        acc = sb("acc", [P, E])
        rk = sb("rk", [P, 2, 2, E])
        rk4 = sb("rk4", [P, 4])
        pos_s = sb("pos_s", [P, 4], I32)
        tok_s = sb("tok_s", [P, 2], I32)
        rank_all = sb("rank_all", [P, 2 * NT])
        ix_all = sb("ix_all", [P, 2 * NT])
        sel = sb("sel", [P, 2 * NT, E])
        base_f = sb("base_f", [P, 2 * NT])
        pos_all = sb("pos_all", [P, NT * 2], I32)
        cmp = sb("cmp", [P, E, NT - 1])
        tl = sb("tl", [P, E])
        cumf = sb("cumf", [P, E + 1])
        cum = sb("cum", [P, E + 1], I32)
        cnt = sb("cnt", [P, E + 1], I32)
        wd = sb("wd", [P, NT])
        we = sb("we", [P, NT])
        ws = sb("ws", [P, NT])
        w_all = sb("w_all", [P, NT, 2])
        idx = sb("idx", [P, 1], I32)
        ctx0 = sb("ctx0", [B, CH])
        ctxx = sb("ctxx", [B, B, CH])
        pos_c = [sb(f"pos_c{j}", [P, 2], I32) for j in range(2)]
        hb = sb("hb", [P, HG])
        st = sb("st", [P, 6])
        mv = sb("mv", [P, 2])
        ve = sb("ve", [P, 1])
        sd = sb("sd", [P, 1])
        rs = sb("rs", [P, 1])
        hn = sb("hn", [P, HG])
        hp = sb("hp", [P, E, HG])
        gl = sb("gl", [P, E])
        gt = sb("gt", [P, E])
        mx2 = sb("mx2", [P, 8])
        ix2 = sb("ix2", [P, 8], U32)
        ixf2 = sb("ixf2", [P, 2])
        mx2_all = sb("mx2_all", [P, NT, 2])
        oh_all = sb("oh_all", [P, NT, 2, E])
        acc2 = sb("acc2", [P, 2 * E])
        allow = sb("allow", [P, 2 * E])
        g2 = sb("g2", [P, NT, 2])
        w2_all = sb("w2_all", [P, NT, E])
        tw = [sb(f"tw{j}", [P, P]) for j in range(2)]
        twt = [sb(f"twt{j}", [P, P]) for j in range(2)]

        s_apart = sem("s_apart")
        s_const = sem("s_const")
        s_zero = sem("s_zero")
        s_x = [sem(f"s_x_{j}") for j in range(2)]
        s_w = [sem(f"s_w_{j}") for j in range(2)]
        s_late = sem("s_late")
        s_pe0 = sem("s_pe0")
        s_act0 = sem("s_act0")
        s_dve0 = sem("s_dve0")
        s_init = sem("s_init")
        s_attx = sem("s_attx")
        s_sm = sem("s_sm")
        s_agg = [sem(f"s_agg_{j}") for j in range(2)]
        s_bd = [sem(f"s_bd_{j}") for j in range(2)]
        s_g = sem("s_g")
        s_gev = sem("s_gev")
        s_l = sem("s_l")
        s_lev = sem("s_lev")
        s_m = sem("s_m")
        s_r = sem("s_r")
        s_rev = sem("s_rev")
        s_c = [sem(f"s_c_{j}") for j in range(2)]
        s_cev = [sem(f"s_cev_{j}") for j in range(2)]
        s_cst = [sem(f"s_cst_{j}") for j in range(2)]
        s_pos = sem("s_pos")
        s_scat = sem("s_scat")
        s_chA = sem("s_chA")
        s_cnt = sem("s_cnt")
        s_cum = sem("s_cum")
        s_chB = sem("s_chB")
        s_wd = sem("s_wd")
        s_we = sem("s_we")
        s_wall = sem("s_wall")
        s_cx = sem("s_cx")
        s_cxx = sem("s_cxx")
        s_cxb = sem("s_cxb")
        s_rest = sem("s_rest")
        s_idx = sem("s_idx")
        s_xg = sem("s_xg")
        s_ta = sem("s_ta")
        s_tb = sem("s_tb")
        s_la = sem("s_la")
        s_lb = sem("s_lb")
        s_fa = sem("s_fa")
        s_h0 = sem("s_h0")
        s_h1 = sem("s_h1")
        s_e0 = sem("s_e0")
        s_e1 = sem("s_e1")
        s_y0 = sem("s_y0")
        s_y1 = sem("s_y1")
        s_pad = sem("s_pad")
        s_pall = sem("s_pall")
        s_pc = sem("s_pc")
        s_yg = [sem(f"s_yg_{j}") for j in range(2)]
        s_xr = [sem(f"s_xr_{j}") for j in range(2)]
        s_chC = sem("s_chC")
        s_x1 = sem("s_x1")
        s_rel = sem("s_rel")
        s_cv = sem("s_cv")
        s_c1 = sem("s_c1")
        s_g1 = sem("s_g1")
        s_g1e = sem("s_g1e")
        s_ve = sem("s_ve")
        s_sd = sem("s_sd")
        s_m0 = sem("s_m0")
        s_m1 = sem("s_m1")
        s_me0 = sem("s_me0")
        s_me1 = sem("s_me1")
        s_a2 = sem("s_a2")
        s_t2 = sem("s_t2")
        s_chD = sem("s_chD")
        s_d2 = sem("s_d2")
        s_ex2 = sem("s_ex2")
        s_tw = sem("s_tw")
        s_twt = sem("s_twt")
        s_twe = sem("s_twe")
        s_lo = sem("s_lo")
        s_fin = sem("s_fin")
        s_out = sem("s_out")

        tile_rows = lambda t: bass.ds(t * P, P)

        block = ctx.enter_context(nc.Block())

        def slots(eng, body):
            with eng.Fori(0, E // 2) as pair:
                for odd in range(2):
                    e = pair * 2 + odd
                    first = eng.value_load(cum[0:1, bass.ds(e, 1)], min_val=0, max_val=SLOTS)
                    count = eng.value_load(cnt[0:1, bass.ds(e, 1)], min_val=1, max_val=NT)
                    with eng.Fori(0, count) as t:
                        body(first + t, t, pair, e, odd)

        def wait_apart(eng, sem_, value):
            eng.wait_ge(sem_, value)
            eng.sem_inc(s_apart, 1)

        @block.sync
        def _(sp):
            for credited in (s_y0, s_y1, s_cst[0], s_cst[1]):
                sp.sem_inc(credited, DMA_CREDIT)
            for credited in (s_e0, s_e1, s_tb, s_g1e, s_me0, s_me1, s_a2, s_twt):
                sp.sem_inc(credited, CREDIT)
            sp.dma_start(ca[:, :], consts_a).then_inc(s_const, 16)
            sp.dma_start(toks[:, :], tok_ids).then_inc(s_const, 16)
            def load_x(rows, j):
                sp.dma_start(x_sb[j], x[rows, :]).then_inc(s_x[j], 16)
                sp.dma_start(xt_sb[j], x_t[rows, :]).then_inc(s_x[j], 16)

            for j in range(2):
                load_x(tile_rows(j), j)
            sp.dma_start(list_d.rearrange("(p n) o -> p (n o)", p=P), zeros).then_inc(s_zero, 16)

            def phase_a(it, row0, last):
                for j in range(2):
                    rows, ahead = (bass.ds(r, P) for r in row0[j])
                    sp.dma_start(w_sb[:, j, bass.ds(it, 1), :],
                                 expert_w[j, bass.ds(it, 1), :, :].rearrange("c p n -> p c n")).then_inc(s_w[j], 16)
                    if not last:
                        sp.wait_ge(s_c[j], it + 1)
                        load_x(ahead, j)
                    sp.wait_ge(s_cev[j], 2 * (it + 1))
                    sp.dma_start(c0_d[rows, :], c0_sb[j]).then_inc(s_cst[j], 16)

            with sp.Fori(0, NT // 2 - 1) as i:
                row0 = [[sp.snap((i * 2 + j + ahead) * P) for ahead in (0, 2)] for j in range(2)]
                phase_a(i, row0, False)
            it = NT // 2 - 1
            phase_a(it, [[(it * 2 + j) * P, 0] for j in range(2)], True)
            sp.dma_start(cb[:, :], consts_b).then_inc(s_late, 16)
            sp.dma_start(conv_sb[:, :, :], conv_w).then_inc(s_late, 16)
            sp.dma_start(down_sb[:, :, :], down_w).then_inc(s_late, 16)
            sp.dma_start(lora_sb[:, :], lora_b).then_inc(s_late, 16)
            sp.dma_start(main_sb[:, :, :], main_w).then_inc(s_late, 16)
            for j in range(2):
                sp.wait_ge(s_cst[j], 16 * (NT // 2) + DMA_CREDIT)
            sp.wait_ge(s_cum, 1)

            def store_slots(e):
                first = sp.value_load(cum[0:1, bass.ds(e, 1)], min_val=0, max_val=SLOTS - 1)
                end = sp.value_load(cum[0:1, bass.ds(e + 1, 1)], min_val=1, max_val=SLOTS)
                with sp.Fori(first, end) as g:
                    rows = bass.ds(sp.snap(g * P), P)
                    sp.wait_ge(s_e0, g + 1 + CREDIT)
                    sp.dma_start(y_d[rows, 0:HALF], yo[:, 0:HALF]).then_inc(s_y0, 16)
                    sp.wait_ge(s_e1, g + 1 + CREDIT)
                    sp.dma_start(y_d[rows, HALF:H], yo[:, HALF:H]).then_inc(s_y1, 16)

            def load_next(e, b):
                nxt = bass.ds(sp.snap(e + 1), 1)
                first = sp.value_load(cum[0:1, bass.ds(e, 1)], min_val=0, max_val=SLOTS)
                sp.wait_ge(s_h1, first)
                for k in range(HC):
                    sp.dma_start(w_sb[:, b, k, :], expert_w[nxt, k, :, :].rearrange("o p n -> p (o n)")).then_inc(s_w[b], 16)

            with sp.Fori(sp.value_load(cum[0:1, E:E + 1], min_val=E, max_val=SLOTS), SLOTS + 1) as g:
                sp.dma_start(y_d[bass.ds(sp.snap(g * P), P), :], c0_sb[0]).then_inc(s_rest, 16)
            store_slots(0)
            with sp.Fori(0, E // 2 - 1) as i:
                for b in range(2):
                    load_next(i * 2 + 1 + b, b)
                    store_slots(i * 2 + 1 + b)
            store_slots(E - 1)

            sp.wait_ge(s_rest, sp.value_load(cnt[0:1, E:E + 1], min_val=1, max_val=SLOTS + 1) * 16)
            for j in range(2):
                sp.dma_start(xr[j], x[tile_rows(j), :]).then_inc(s_xr[j], 16)
            with sp.Fori(1, NT // 2) as i:
                for j in range(2):
                    rows = bass.ds(sp.snap((i * 2 + j) * P), P)
                    sp.wait_ge(s_x1, i * 2 + j - 1)
                    sp.dma_start(xr[j], x[rows, :]).then_inc(s_xr[j], 16)
            with sp.Fori(0, NT) as t:
                rows = bass.ds(sp.snap(t * P), P)
                at = sp.snap(t * 1)
                sp.wait_ge(s_fin, (t + 1) * 2)
                sp.dma_start(out[rows, :], res[:, bass.ds(at, 1), :].rearrange("p o n -> p (o n)")).then_inc(s_out, 16)
            sp.wait_ge(s_out, 16 * NT)

        @block.gpsimd
        def _(pool):
            for j in range(2):
                pool.memset(bd[j][:, :], 0.0).then_inc(s_init, 1)
            for j in range(2):
                for a in (0, MW - PAD // 2):
                    pool.memset(x1p[j][:, :, a:a + PAD // 2], 0.0).then_inc(s_pad, 1)
            pool.memset(acc[:, :], 0.0).then_inc(s_init, 1)
            pool.memset(acc2[:, :], 0.0).then_inc(s_init, 1)
            pool.memset(cumf[:, 0:1], 0.0).then_inc(s_init, 1)
            pool.wait_ge(s_zero, 16)
            with pool.Fori(0, NT // 2) as it:
                wait_apart(pool, s_pos, it + 1)
                for j in range(2):
                    for k in range(2):
                        pool.indirect_dma_start(list_d, bass.IndirectOffsetOnAxis(ap=pos_s[:, 2 * j + k:2 * j + k + 1], axis=0),
                                                tok_s[:, j:j + 1], None).then_inc(s_scat, 16)
            pool.wait_ge(s_scat, 16 * 2 * NT)
            for j in range(2):
                pool.wait_ge(s_cst[j], 16 * (NT // 2) + DMA_CREDIT)
            pool.wait_ge(s_cum, 1)

            def gather():
                pool.indirect_dma_start(xg, None, c0_d, bass.IndirectOffsetOnAxis(ap=idx[:, 0:1], axis=0)).then_inc(s_xg, 16)

            def slot(g, t, pair, e, odd):
                rows = bass.ds(pool.snap(t * P + e * N), P)
                pool.dma_start(idx[:, :], list_d[rows, :]).then_inc(s_idx, 16)
                wait_apart(pool, s_idx, (g + 1) * 16)
                wait_apart(pool, s_tb, g + CREDIT)
                gather()
                wait_apart(pool, s_xg, (g + 1) * 16)

            slots(pool, slot)
            total = pool.value_load(cum[0:1, E:E + 1], min_val=E, max_val=SLOTS)
            wait_apart(pool, s_tb, total + CREDIT)
            gather()
            pool.wait_ge(s_pall, 1)
            wait_apart(pool, s_y0, total * 16 + DMA_CREDIT)
            wait_apart(pool, s_y1, total * 16 + DMA_CREDIT)


            def fetch(t, j, it):
                pool.tensor_copy(pos_c[j][:, :], pos_all[:, bass.ds(t * 2, 2)]).then_inc(s_pc, 1)
                wait_apart(pool, s_pc, t + 1)
                for k in range(2):
                    pool.indirect_dma_start(yg[j][:, k, :], None, y_d,
                                            bass.IndirectOffsetOnAxis(ap=pos_c[j][:, k:k + 1], axis=0)).then_inc(s_yg[j], 16)

            fetch(0, 0, 0)
            fetch(1, 1, 0)
            with pool.Fori(1, NT // 2) as i:
                for j in range(2):
                    wait_apart(pool, s_x1, i * 2 + j - 1)
                    fetch(i * 2 + j, j, i)

        @block.scalar
        def _(act):
            act.wait_ge(s_const, 32)
            act.wait_ge(s_pe0, 1)
            act.activation(h0[:, :], bank[0][:, 0:B], ACT.Gelu, bias=c("b0")).then_inc(s_act0, 1)
            act.wait_ge(s_pe0, 4)
            act.activation(h1[:, :], bank[1][:, 0:B], ACT.Gelu, bias=c("b1")).then_inc(s_act0, 1)
            act.wait_ge(s_sm, 1)
            act.activation(at_e[:, :], at_l[:, :], ACT.Exp, bias=at_n[:, :], accum_out=at_s[:, :]).then_inc(s_act0, 1)

            def spread(j, it):
                act.wait_ge(s_agg[j], it + 1)
                act.activation(bd[j][0:CH, 0:CH], agg[j][0:CH, :], ACT.Copy).then_inc(s_bd[j], 1)
                act.activation(bd[j][CH:P, CH:P], agg[j][CH:P, :], ACT.Copy).then_inc(s_bd[j], 1)

            act.wait_ge(s_init, 5)
            for j in range(2):
                spread(j, 0)

            def phase_a(it, last):
                for j in range(2):
                    act.wait_ge(s_c[j], it + 1)
                    if not last:
                        spread(j, it + 1)
                    act.wait_ge(s_cst[j], it * 16 + DMA_CREDIT)
                    for h in range(2):
                        act.activation(c0_sb[j][:, h * HALF:(h + 1) * HALF], bank[2 * j + h][:, :], ACT.Identity,
                                       bias=aggb[:, bass.ds(it * 2 + j, 1)]).then_inc(s_cev[j], 1)

            with act.Fori(0, NT // 2 - 1) as it:
                phase_a(it, False)
            phase_a(NT // 2 - 1, True)
            act.wait_ge(s_wd, 1)
            act.activation(we[:, :], wd[:, :], ACT.Exp).then_inc(s_we, 1)
            act.wait_ge(s_cum, 1)

            def slot(g, t, pair, e, odd):
                act.wait_ge(s_h0, g + 1)
                act.wait_ge(s_y0, g * 16 + DMA_CREDIT)
                act.activation(yo[:, 0:HALF], bank[0][:, :], ACT.Copy).then_inc(s_e0, 1)
                act.wait_ge(s_h1, g + 1)
                act.wait_ge(s_y1, g * 16 + DMA_CREDIT)
                act.activation(yo[:, HALF:H], bank[1][:, :], ACT.Copy).then_inc(s_e1, 1)

            slots(act, slot)

            act.wait_ge(s_pad, 4)

            def rearrange(t, j, free):
                act.wait_ge(s_x1, t + 1)
                if free is not None:
                    act.wait_ge(s_cv, free)
                for b in range(2):
                    rows = res[b * CH:(b + 1) * CH, bass.ds(t, 1), :].rearrange("p o (m q) -> p (o m) q", q=2)
                    for q in range(2):
                        act.activation(x1p[j][q * CH:(q + 1) * CH, b, PAD // 2:PAD // 2 + HALF], rows[:, :, q],
                                       ACT.Copy).then_inc(s_rel, 1)

            def root(t):
                act.wait_ge(s_ve, t + 1)
                act.activation(sd[:, :], ve[:, :], ACT.Sqrt).then_inc(s_sd, 1)

            rearrange(0, 0, None)
            rearrange(1, 1, None)
            with act.Fori(0, NT // 2 - 1) as i:
                for j in range(2):
                    root(i * 2 + j)
                    rearrange(i * 2 + j + 2, j, (i * 2 + j + 1) * 2)
            for t in range(NT - 2, NT):
                root(t)
            act.wait_ge(s_d2, 1)
            act.activation(we[:, :], wd[:, :], ACT.Exp).then_inc(s_ex2, 1)
            with act.Fori(0, NT // 2) as i:
                for j in range(2):
                    t = i * 2 + j
                    act.wait_ge(s_twt, t + 1 + CREDIT)
                    act.activation(twt[j][:, :], bank[4 + j][:, 0:P], ACT.Copy).then_inc(s_twe, 1)

        @block.vector
        def _(dve):
            ch = Chain(dve, s_dve0)
            dve.wait_ge(s_const, 32)
            dve.wait_ge(s_pe0, 2)
            ch.add(dve.tensor_copy(gsum[:, :], bank[2][:, 0:E]))
            dve.wait_ge(s_pe0, 3)
            ch.link(dve.tensor_copy(ctx0[:, :], bank[3][0:B, 0:CH]))
            dve.wait_ge(s_pe0, 5)
            ch.link(dve.tensor_tensor(at_l[:, :], bank[4][0:B, 0:K8], c("b2", B), ALU.add))
            ch.link(dve.tensor_reduce(at_m[:, :], at_l[:, :], AX.X, ALU.max))
            dve.tensor_scalar(at_n[:, :], at_m[:, :], -1.0, None, ALU.mult).then_inc(s_sm, 1)
            dve.wait_ge(s_act0, 3)
            ch.link(dve.reciprocal(at_r[:, :], at_s[:, :]))
            ch.link(dve.tensor_scalar(att[:, :], at_e[:, :], at_r[:, 0:1], None, ALU.mult))
            dve.tensor_tensor(attx[:, :, :], c("ident", B)[:, 0:B].unsqueeze(2).to_broadcast([B, B, K8]),
                              att[:, :].unsqueeze(1).to_broadcast([B, B, K8]), ALU.mult).then_inc(s_attx, 1)
            dve.wait_ge(s_pe0, 6)
            spread = bank[5][:, 0:B * K8].rearrange("p (t q k) -> p t q k", q=2, k=K8)
            attp3 = attp[:, :].rearrange("p (t k) -> p t k", k=K8)
            for q in range(2):
                ch.add(dve.tensor_copy(attp3[q * CH:(q + 1) * CH, :, :], spread[q * CH:(q + 1) * CH, :, q, :]))
            ch.wait()
            ch.link(dve.tensor_tensor(aggb_t[:, :, :], attp3, c("kbias").unsqueeze(1).to_broadcast([P, NT, K8]), ALU.mult))
            ch.link(dve.tensor_reduce(aggb[:, :], aggb_t[:, :, :], AX.X, ALU.add))

            kern = c("kern").rearrange("p (k o) -> p k o", k=K8)

            def aggregate(ch, it, free):
                if free is not None:
                    for j in range(2):
                        dve.wait_ge(s_bd[j], free)
                last = [0, 0]
                for k in range(K8):
                    for j in range(2):
                        w = attp[:, bass.ds((it * 2 + j) * K8 + k, 1)]
                        if k == 0:
                            ins = dve.tensor_scalar(agg[j][:, :], kern[:, k, :], w, None, ALU.mult)
                        else:
                            ch.wait(last[j])
                            ins = dve.scalar_tensor_tensor(agg[j][:, :], kern[:, k, :], w, agg[j][:, :], ALU.mult, ALU.add)
                        if k == K8 - 1:
                            ins.then_inc(s_agg[j], 1)
                        else:
                            last[j] = ch.add(ins)

            aggregate(ch, 0, None)

            oh4 = oh[:, :, :, :].rearrange("p j k e -> p (j k) e")
            rk4v = rk[:, :, :, :].rearrange("p j k e -> p (j k) e")
            iota4 = c("iota").unsqueeze(1).to_broadcast([P, 4, E])

            def take_gate(it):
                dve.wait_ge(s_g, it + 1)
                dve.wait_ge(s_l, it)
                dve.tensor_copy(g_sb[:, :], bank[4][:, 0:2 * E]).then_inc(s_gev, 1)

            def place(ch, it, first=False):
                dve.wait_ge(s_r, it + 1)
                ranks = bank[6][:, 0:2 * E].rearrange("p (j e) -> p j e", j=2)
                for k in range(2):
                    n = ch.add(dve.tensor_tensor(rk[:, :, k, :], oh[:, :, k, :], ranks, ALU.mult))
                ch.wait(n)
                ch.link(dve.tensor_reduce(rk4[:, :], rk4v, AX.X, ALU.add))
                if not first:
                    dve.wait_ge(s_scat, it * 64)
                ch.add(dve.tensor_copy(tok_s[:, :], toks[:, bass.ds(it * 2, 2)]))
                ch.add(dve.tensor_copy(rank_all[:, bass.ds(it * 4, 4)], rk4[:, :]))
                ch.add(dve.tensor_copy(ix_all[:, bass.ds(it * 4, 4)], ixf[:, :]))
                ch.wait()
                dve.scalar_tensor_tensor(pos_s[:, :], ixf[:, :], float(N), rk4[:, :], ALU.mult, ALU.add).then_inc(s_pos, 1)

            def route(ch, it):
                dve.wait_ge(s_l, it + 1)
                for j in range(2):
                    n = ch.add(dve.scalar_tensor_tensor(lg[:, j, :], gsum[:, :], aggb[:, bass.ds(it * 2 + j, 1)],
                                                        bank[5][:, j * E:(j + 1) * E], ALU.mult, ALU.add))
                wait_apart(dve, s_chA, ch.base + n)
                for j in range(2):
                    n = ch.add(dve.max(mx[:, j, :], lg[:, j, :]))
                ch.wait(n)
                ch.add(dve.tensor_copy(mx_all[:, bass.ds(it * 2, 2), :], mx[:, :, 0:2]))
                for j in range(2):
                    ch.add(dve.max_index(ix[:, j, :], mx[:, j, :], lg[:, j, :]))
                ch.wait()
                ch.link(dve.tensor_copy(ixf[:, :].rearrange("p (j k) -> p j k", j=2), ix[:, :, 0:2]))
                ch.link(dve.tensor_tensor(oh4, iota4, ixf[:, :].unsqueeze(2).to_broadcast([P, 4, E]), ALU.is_equal))
                dve.wait_ge(s_m, it)
                ch.add(dve.tensor_copy(pre[:, 0, :], acc[:, :]))
                ch.link(dve.tensor_tensor(msk[:, :, :], oh[:, :, 0, :], oh[:, :, 1, :], ALU.add))
                ch.link(dve.tensor_tensor(pre[:, 1, :], pre[:, 0, :], msk[:, 0, :], ALU.add))
                dve.tensor_tensor(acc[:, :], pre[:, 1, :], msk[:, 1, :], ALU.add).then_inc(s_m, 1)

            LA = 32
            dve.wait_ge(s_init, 5)
            take_gate(0)
            ca0 = Chain(dve, s_chA)
            route(ca0, 0)
            aggregate(ca0, 1, 2)
            take_gate(1)
            place(ca0, 0, True)
            route(ca0, 1)
            aggregate(ca0, 2, 4)
            base = ca0.n
            with dve.Fori(2, NT // 2 - 1) as it:
                ch = Chain(dve, s_chA, (it - 2) * LA + base)
                take_gate(it)
                place(ch, it - 1)
                route(ch, it)
                aggregate(ch, it + 1, (it + 1) * 2)
                assert ch.n == LA, ch.n
            ch = Chain(dve, s_chA, base + LA * (NT // 2 - 3))
            it = NT // 2 - 1
            take_gate(it)
            place(ch, it - 1)
            route(ch, it)
            place(ch, it)

            ch = Chain(dve, s_chB)
            dve.wait_ge(s_cnt, 1)
            ch.link(dve.tensor_tensor(cmp[:, :, :], bank[4][:, 0:E].unsqueeze(2).to_broadcast([P, E, NT - 1]),
                                      c("thr").unsqueeze(1).to_broadcast([P, E, NT - 1]), ALU.is_gt))
            ch.link(dve.tensor_reduce(tl[:, :], cmp[:, :, :], AX.X, ALU.add))
            for e in range(E):
                ch.link(dve.scalar_tensor_tensor(cumf[:, e + 1:e + 2], tl[:, e:e + 1], 1.0, cumf[:, e:e + 1], ALU.add, ALU.add))
            ch.add(dve.tensor_scalar(cnt[:, 0:E], tl[:, :], 1.0, None, ALU.add))
            ch.link(dve.tensor_scalar(cnt[:, E:E + 1], cumf[:, E:E + 1], -1.0, float(SLOTS + 1), ALU.mult, ALU.add))
            dve.tensor_copy(cum[:, :], cumf[:, :]).then_inc(s_cum, 1)
            def turn(g):
                dve.wait_ge(s_ta, g + 1)
                dve.wait_ge(s_fa, g)
                dve.tensor_copy(lhs[:, 0:4, :], bank[2][:, :].rearrange("p (c m) -> p c m", c=4)).then_inc(s_la, 1)
                dve.wait_ge(s_tb, g + 1 + CREDIT)
                dve.wait_ge(s_h1, g)
                dve.tensor_copy(lhs[:, 4:8, :], bank[3][:, :].rearrange("p (c m) -> p c m", c=4)).then_inc(s_lb, 1)

            dve.tensor_tensor(ctxx[:, :, :], c("ident", B)[:, 0:B].unsqueeze(2).to_broadcast([B, B, CH]),
                              ctx0[:, :].unsqueeze(1).to_broadcast([B, B, CH]), ALU.mult).then_inc(s_cxx, 1)
            turn(0)
            dve.tensor_tensor(wd[:, :], mx_all[:, :, 1], mx_all[:, :, 0], ALU.subtract).then_inc(s_wd, 1)
            dve.wait_ge(s_we, 1)
            ch.link(dve.tensor_scalar(ws[:, :], we[:, :], 1.0, None, ALU.add))
            ch.link(dve.reciprocal(w_all[:, :, 0], ws[:, :]))
            ch.link(dve.tensor_tensor(w_all[:, :, 1], we[:, :], w_all[:, :, 0], ALU.mult))
            dve.wait_ge(s_cxb, 1)
            ctx4 = ctxb[:, :, :].rearrange("p (q n) o -> p q n o", q=4)
            for q in range(4):
                dve.tensor_tensor(ctx4[:, q], bank[4 + q][:, :].rearrange("p (n o) -> p n o", o=CH),
                                  c("fside").unsqueeze(1).to_broadcast([P, B // 4, CH]), ALU.add).then_inc(s_cx, 1)
            ch.link(dve.tensor_tensor(sel[:, :, :], c("iota").unsqueeze(1).to_broadcast([P, 2 * NT, E]),
                                      ix_all[:, :].unsqueeze(2).to_broadcast([P, 2 * NT, E]), ALU.is_equal))
            ch.link(dve.tensor_tensor(sel[:, :, :], sel[:, :, :],
                                      cumf[:, 0:E].unsqueeze(1).to_broadcast([P, 2 * NT, E]), ALU.mult))
            ch.link(dve.tensor_reduce(base_f[:, :], sel[:, :, :], AX.X, ALU.add))
            dve.scalar_tensor_tensor(pos_all[:, :], base_f[:, :], float(P), rank_all[:, :], ALU.mult, ALU.add).then_inc(s_pall, 1)

            slots(dve, lambda g, t, pair, e, odd: turn(g + 1))

            dve.wait_ge(s_late, 80)
            dve.wait_ge(s_cx, 4)

            LC = 16
            def combine(ch, t, j, it):
                dve.wait_ge(s_yg[j], (it + 1) * 32)
                dve.wait_ge(s_xr[j], (it + 1) * 16)
                rows = res[:, bass.ds(t, 1), :].rearrange("p o n -> p (o n)")
                w2 = w_all[:, bass.ds(t, 1), :].rearrange("p o k -> p (o k)")
                ch.link(dve.scalar_tensor_tensor(rows, yg[j][:, 0, :], w2[:, 0:1], xr[j], ALU.mult, ALU.add))
                dve.scalar_tensor_tensor(rows, yg[j][:, 1, :], w2[:, 1:2], rows, ALU.mult, ALU.add).then_inc(s_x1, 1)

            def take_conv(t, j):
                out5 = c1[j].rearrange("p (q c) (b o) -> p b c q o", q=2, b=2)
                for b in range(2):
                    dve.wait_ge(s_cv, t * 2 + b + 1)
                    add = ctxb[:, bass.ds(t * 2 + b, 1), :].rearrange("p n o -> p (n o)").unsqueeze(1).to_broadcast([P, 4, CH])
                    ps = bank[4 + b][:, :].rearrange("p (c q o) -> p q c o", c=4, q=2)
                    for q in range(2):
                        dve.tensor_tensor(out5[:, b, :, q, :], ps[:, q], add, ALU.add).then_inc(s_c1, 1)

            def gate(ch, t):
                dve.wait_ge(s_g1, t + 1)
                down = down_all[:, bass.ds(t, 1), :].rearrange("p o n -> p (o n)")
                ins = dve.tensor_copy(down, bank[2][:, 0:G1W])
                ins.then_inc(s_g1e, 1)
                dve.wait_ge(s_g1e, t + 1 + CREDIT)
                ch.link(dve.tensor_tensor(hb[:, :], down[:, E * R:G1W], d("gb1"), ALU.add))
                ch.add(dve.bn_stats(st[:, :], hb[:, :]))
                wait_apart(dve, s_chC, ch.base + ch.n)
                ch.link(dve.bn_aggr(mv[:, :], st[:, :]))
                dve.tensor_scalar(ve[:, :], mv[:, 1:2], LN_EPS, None, ALU.add).then_inc(s_ve, 1)
                dve.wait_ge(s_sd, t + 1)
                ch.link(dve.reciprocal(rs[:, :], sd[:, :]))
                ch.link(dve.tensor_scalar(hn[:, :], hb[:, :], mv[:, 0:1], rs[:, 0:1], ALU.subtract, ALU.mult))
                ch.link(dve.tensor_tensor(hb[:, :], hn[:, :], d("gamma"), ALU.mult))
                ch.link(dve.tensor_tensor(hn[:, :], hb[:, :], d("beta"), ALU.add))
                ch.link(dve.scalar_tensor_tensor(hp[:, :, :], hn[:, :].unsqueeze(1).to_broadcast([P, E, HG]), 0.0,
                                                 d("gw2").rearrange("p (e h) -> p e h", e=E), ALU.max, ALU.mult))
                ch.link(dve.tensor_reduce(gl[:, :], hp[:, :, :], AX.X, ALU.add))
                ch.add(dve.tensor_tensor(gt[:, :], gl[:, :], d("gb2"), ALU.add))
                wait_apart(dve, s_chC, ch.base + ch.n)
                ch.link(dve.max(mx2[:, :], gt[:, :]))
                ch.add(dve.tensor_copy(mx2_all[:, bass.ds(t, 1), :].rearrange("p o k -> p (o k)"), mx2[:, 0:2]))
                ch.link(dve.max_index(ix2[:, :], mx2[:, :], gt[:, :]))
                ch.link(dve.tensor_copy(ixf2[:, :], ix2[:, 0:2]))
                ohv = oh_all[:, bass.ds(t, 1), :, :].rearrange("p o k e -> p (o k) e")
                ch.link(dve.tensor_tensor(ohv, c("iota").unsqueeze(1).to_broadcast([P, 2, E]),
                                          ixf2[:, :].unsqueeze(2).to_broadcast([P, 2, E]), ALU.is_equal))
                acc2v = acc2[:, :].rearrange("p (k e) -> p k e", k=2)
                dve.wait_ge(s_a2, t + CREDIT)
                dve.tensor_tensor(acc2v, acc2v, ohv, ALU.add).then_inc(s_a2, 1)

            def take_main(t):
                rows = res[:, bass.ds(t, 1), :].rearrange("p o n -> p (o n)")
                for h, (s, done) in enumerate(((s_m0, s_me0), (s_m1, s_me1))):
                    dve.wait_ge(s, t + 1)
                    half = rows[:, h * HALF:(h + 1) * HALF]
                    dve.tensor_tensor(half, bank[h][:, :], half, ALU.add).then_inc(done, 1)

            ch = Chain(dve, s_chC)
            combine(ch, 0, 0, 0)
            combine(ch, 1, 1, 0)
            take_conv(0, 0)
            with dve.Fori(0, NT // 2 - 1) as i:
                ch = Chain(dve, s_chC, i * (2 * LC) + 2)
                for j in range(2):
                    t = i * 2 + j
                    take_conv(t + 1, 1 - j)
                    gate(ch, t)
                    combine(ch, t + 2, j, i + 1)
                    take_main(t)
                assert ch.n == 2 * LC, ch.n
            ch = Chain(dve, s_chC, (NT // 2 - 1) * 2 * LC + 2)
            take_conv(NT - 1, 1)
            gate(ch, NT - 2)
            take_main(NT - 2)
            gate(ch, NT - 1)
            take_main(NT - 1)

            ch = Chain(dve, s_chD)
            dve.tensor_tensor(wd[:, :], mx2_all[:, :, 1], mx2_all[:, :, 0], ALU.subtract).then_inc(s_d2, 1)
            dve.wait_ge(s_ex2, 1)
            ch.link(dve.tensor_scalar(ws[:, :], we[:, :], 1.0, None, ALU.add))
            ch.link(dve.reciprocal(g2[:, :, 0], ws[:, :]))
            ch.link(dve.tensor_tensor(g2[:, :, 1], we[:, :], g2[:, :, 0], ALU.mult))
            dve.wait_ge(s_t2, 1)
            ch.link(dve.tensor_scalar(allow[:, :], bank[2][:, 0:2 * E], float(CAPACITY), None, ALU.is_le))
            oh_t = oh_all[:, :, :, :].rearrange("p t k e -> p t (k e)")
            oh_k = oh_all[:, :, :, :].rearrange("p t k e -> p (t k) e")
            ch.link(dve.tensor_tensor(oh_t, oh_t, allow[:, :].unsqueeze(1).to_broadcast([P, NT, 2 * E]), ALU.mult))
            g2v = g2[:, :, :].rearrange("p t k -> p (t k)").unsqueeze(2).to_broadcast([P, 2 * NT, E])
            ch.link(dve.tensor_tensor(oh_k, oh_k, g2v, ALU.mult))
            ch.link(dve.tensor_tensor(w2_all[:, :, :], oh_all[:, :, 0, :], oh_all[:, :, 1, :], ALU.add))

            def weigh(t, j):
                down = down_all[:, bass.ds(t, 1), 0:E * R].rearrange("p o (e r) -> p (o e) r", r=R)
                w = w2_all[:, bass.ds(t, 1), :].rearrange("p o e -> p (o e)").unsqueeze(2).to_broadcast([P, E, R])
                dve.scalar_tensor_tensor(tw[j][:, :].rearrange("p (e r) -> p e r", r=R), down, ALPHA, w,
                                         ALU.mult, ALU.mult).then_inc(s_tw, 1)

            def finish(t, j):
                rows = res[:, bass.ds(t, 1), :].rearrange("p o n -> p (o n)")
                for h in range(2):
                    dve.wait_ge(s_lo, t * 2 + h + 1)
                    half = rows[:, h * HALF:(h + 1) * HALF]
                    dve.tensor_tensor(half, bank[2 * j + h][:, :], half, ALU.add).then_inc(s_fin, 1)

            weigh(0, 0)
            with dve.Fori(0, NT // 2 - 1) as i:
                for j in range(2):
                    t = i * 2 + j
                    dve.wait_ge(s_twt, t + CREDIT)
                    weigh(t + 1, 1 - j)
                    finish(t, j)
            dve.wait_ge(s_twt, NT - 2 + CREDIT)
            weigh(NT - 1, 1)
            finish(NT - 2, 0)
            finish(NT - 1, 1)

        @block.tensor
        def _(pe):
            ones = c("ones")
            ident = c("ident")
            gatec = c("gate").rearrange("p (c e) -> p c e", c=HC)
            pe.wait_ge(s_const, 32)
            pe.matmul(bank[0][:, 0:B], c("w0"), c("emb"), start=True, stop=True).then_inc(s_pe0, 1)
            for k in range(HC):
                mm = pe.matmul(bank[2][:, 0:E], ones, gatec[:, k, :], start=(k == 0), stop=(k == HC - 1))
            mm.then_inc(s_pe0, 1)
            pe.matmul(bank[3][0:B, 0:CH], c("emb"), c("cw"), start=True, stop=True).then_inc(s_pe0, 1)
            pe.wait_ge(s_act0, 1)
            pe.matmul(bank[1][:, 0:B], c("w1"), h0[:, :], start=True, stop=True).then_inc(s_pe0, 1)
            pe.wait_ge(s_act0, 2)
            pe.matmul(bank[4][0:B, 0:K8], h1[:, :], c("w2"), start=True, stop=True).then_inc(s_pe0, 1)
            pe.wait_ge(s_attx, 1)
            pe.matmul(bank[5][:, 0:B * K8], c("ones", B), attx[:, :, :].rearrange("p n k -> p (n k)"),
                      start=True, stop=True).then_inc(s_pe0, 1)
            pe.wait_ge(s_agg[0], 1)

            def ranks(it):
                pe.wait_ge(s_m, it + 1)
                pe.matmul(bank[6][:, 0:2 * E], c("tri"), msk[:, :, :].rearrange("p j e -> p (j e)"), start=True, stop=False)
                pe.matmul(bank[6][:, 0:2 * E], ones, pre[:, :, :].rearrange("p j e -> p (j e)"),
                          start=False, stop=True).then_inc(s_r, 1)

            def phase_a(it, first):
                pe.wait_ge(s_gev, it)
                for j in range(2):
                    pe.wait_ge(s_x[j], (it + 1) * 32)
                    for k in range(HC):
                        mm = pe.matmul(bank[4][:, j * E:(j + 1) * E], xt_sb[j][:, k * P:(k + 1) * P], gatec[:, k, :],
                                       start=(k == 0), stop=(k == HC - 1))
                mm.then_inc(s_g, 1)
                if not first:
                    ranks(it - 1)
                pe.wait_ge(s_gev, it + 1)
                for j in range(2):
                    pe.wait_ge(s_bd[j], (it + 1) * 2)
                    mm = pe.matmul(bank[5][:, j * E:(j + 1) * E], bd[j][:, :], g_sb[:, j * E:(j + 1) * E], start=True, stop=True)
                mm.then_inc(s_l, 1)
                for j in range(2):
                    pe.wait_ge(s_cev[j], it * 2)
                    for h in range(2):
                        mm = pe.matmul(bank[2 * j + h][:, :], bd[j][:, :], x_sb[j][:, h * HALF:(h + 1) * HALF], start=True, stop=True)
                    mm.then_inc(s_c[j], 1)

            phase_a(0, True)
            with pe.Fori(1, NT // 2) as it:
                phase_a(it, False)
            ranks(NT // 2 - 1)
            pe.wait_ge(s_gev, NT // 2)
            pe.matmul(bank[4][:, 0:E], ones, acc[:, :], start=True, stop=True).then_inc(s_cnt, 1)
            pe.wait_ge(s_cxx, 1)
            for q in range(4):
                mm = pe.matmul(bank[4 + q][:, :], c("ones", B),
                               ctxx[:, q * 8:(q + 1) * 8, :].rearrange("p n o -> p (n o)"), start=True, stop=True)
            mm.then_inc(s_cxb, 1)

            for j in range(2):
                pe.wait_ge(s_cev[j], NT)

            def transposes(g):
                pe.wait_ge(s_xg, (g + 1) * 16)
                for half, (bk, s) in enumerate(((2, s_ta), (3, s_tb))):
                    for k in range(4):
                        at = half * 4 + k
                        mm = pe.transpose(bank[bk][:, k * P:(k + 1) * P], xg[:, at * P:(at + 1) * P], ident)
                    mm.then_inc(s, 1)

            transposes(0)
            pe.wait_ge(s_cum, 1)

            def slot(g, t, pair, e, odd):
                pe.wait_ge(s_w[odd], (pair + 1) * (HC * 16))
                pe.wait_ge(s_e0, g + CREDIT)
                pe.wait_ge(s_la, g + 1)
                for k in range(HC):
                    if k == 4:
                        pe.wait_ge(s_lb, g + 1)
                    mm = pe.matmul(bank[0][:, :], lhs[:, k, :], w_sb[:, odd, k, 0:HALF], start=(k == 0), stop=(k == HC - 1))
                mm.then_inc(s_h0, 1)
                transposes(g + 1)
                pe.wait_ge(s_e1, g + CREDIT)
                for k in range(HC):
                    mm = pe.matmul(bank[1][:, :], lhs[:, k, :], w_sb[:, odd, k, HALF:H], start=(k == 0), stop=(k == HC - 1))
                    if k == 3:
                        mm.then_inc(s_fa, 1)
                mm.then_inc(s_h1, 1)

            slots(pe, slot)

            total = pe.value_load(cum[0:1, E:E + 1], min_val=E, max_val=SLOTS)
            pe.wait_ge(s_late, 80)
            pe.wait_ge(s_cx, 4)
            pe.wait_ge(s_e0, total + CREDIT)
            pe.wait_ge(s_e1, total + CREDIT)
            wait_apart(pe, s_lb, total + 1)

            def conv(t, j, rel, free):
                pe.wait_ge(s_rel, rel)
                if free is not None:
                    pe.wait_ge(s_c1, free)
                for b in range(2):
                    for m in range(4):
                        for k in range(PAIRS):
                            mm = pe.matmul(bank[4 + b][:, m * P:(m + 1) * P], x1p[j][:, b, m * P + k:(m + 1) * P + k],
                                           conv_sb[:, k, :], start=(k == 0), stop=(k == PAIRS - 1))
                    mm.then_inc(s_cv, 1)

            def products(t, j):
                pe.wait_ge(s_c1, (t + 1) * 4)
                pe.wait_ge(s_g1e, t + CREDIT)
                for k in range(HC):
                    mm = pe.matmul(bank[2][:, 0:G1W], c1[j][:, k, :], down_sb[:, k, :], start=(k == 0), stop=(k == HC - 1))
                mm.then_inc(s_g1, 1)
                for h, (s, done) in enumerate(((s_m0, s_me0), (s_m1, s_me1))):
                    pe.wait_ge(done, t + CREDIT)
                    for k in range(HC):
                        mm = pe.matmul(bank[h][:, :], c1[j][:, k, :], main_sb[:, k, h * HALF:(h + 1) * HALF],
                                       start=(k == 0), stop=(k == HC - 1))
                    mm.then_inc(s, 1)

            conv(0, 0, 4, None)
            with pe.Fori(0, NT // 2 - 1) as i:
                for j in range(2):
                    t = i * 2 + j
                    conv(t + 1, 1 - j, (t + 2) * 4, (t + 1) * 4)
                    products(t, j)
            conv(NT - 1, 1, NT * 4, (NT - 1) * 4)
            products(NT - 2, 0)
            products(NT - 1, 1)
            pe.wait_ge(s_a2, NT + CREDIT)
            pe.matmul(bank[2][:, 0:2 * E], ones, acc2[:, :], start=True, stop=True).then_inc(s_t2, 1)

            def turn(t, j):
                pe.wait_ge(s_tw, t + 1)
                pe.transpose(bank[4 + j][:, 0:P], tw[j][:, :], ident).then_inc(s_twt, 1)

            def lora(t, j, free):
                pe.wait_ge(s_twe, t + 1)
                pe.wait_ge(s_fin, free)
                for h in range(2):
                    pe.matmul(bank[2 * j + h][:, :], twt[j][:, :], lora_sb[:, h * HALF:(h + 1) * HALF],
                              start=True, stop=True).then_inc(s_lo, 1)

            pe.wait_ge(s_me1, NT + CREDIT)
            turn(0, 0)
            turn(1, 1)
            lora(0, 0, 0)
            turn(2, 0)
            lora(1, 1, 0)
            with pe.Fori(1, NT // 2 - 1) as i:
                for j in range(2):
                    t = i * 2 + j
                    turn(t + 1, 1 - j)
                    lora(t, j, (t - 1) * 2)
            turn(NT - 1, 1)
            lora(NT - 2, 0, (NT - 3) * 2)
            lora(NT - 1, 1, (NT - 2) * 2)


INPUTS = ["x", "x_t", "consts_a", "consts_b", "tok_ids", "zeros", "expert_w", "conv_w", "down_w", "main_w", "lora_b"]


def lay_out(i):
    f = np.float32
    a = np.zeros((P, CA_W), f)
    b = np.zeros((P, CB_W), f)

    def put(to, where, name, v):
        lo, hi = where[name]
        to[:, lo:hi] = np.reshape(v, (-1, hi - lo)) if np.ndim(v) else v

    put(a, CA, "emb", i["cond_128"].T)
    put(a, CA, "w0", i["L0_cond_W0"])
    put(a, CA, "w1", i["L0_cond_W1"])
    put(a, CA, "w2", i["L0_cond_W2"])
    put(a, CA, "b0", i["L0_cond_b0"][:, None])
    put(a, CA, "b1", i["L0_cond_b1"][:, None])
    put(a, CA, "b2", np.broadcast_to(i["L0_cond_b2"], (P, K8)))
    put(a, CA, "gate", i["L0_ffn_gate_w"].reshape(HC, P, E).transpose(1, 0, 2).reshape(P, -1))
    kern = i["L0_cond_weight"][..., 0].transpose(2, 0, 1).reshape(CH, -1)
    put(a, CA, "kern", np.concatenate([kern, kern]))
    put(a, CA, "kbias", np.concatenate([i["L0_cond_bias_k"].T] * 2))
    put(a, CA, "ident", np.eye(P, dtype=f))
    put(a, CA, "tri", np.triu(np.ones((P, P), f), 1))
    put(a, CA, "ones", np.ones((P, P), f))
    put(a, CA, "iota", np.broadcast_to(np.arange(E, dtype=f), (P, E)))
    put(a, CA, "thr", np.broadcast_to(np.arange(1, NT, dtype=f) * P, (P, NT - 1)))
    put(a, CA, "cw", i["L1_cond_c_weight"].T)
    put(a, CA, "fside", np.broadcast_to(i["fside_S_0"], (P, CH)))
    put(b, CB, "gb1", np.broadcast_to(i["L1_ffn_gb1"], (P, HG)))
    put(b, CB, "gamma", np.broadcast_to(i["L1_ffn_ln_gamma"], (P, HG)))
    put(b, CB, "beta", np.broadcast_to(i["L1_ffn_ln_beta"], (P, HG)))
    put(b, CB, "gb2", np.broadcast_to(i["L1_ffn_gb2"], (P, E)))
    put(b, CB, "gw2", np.broadcast_to(i["L1_ffn_gw2"].reshape(-1), (P, E * HG)))

    w = i["L1_cond_weight"]
    per = w.shape[1]
    conv = np.zeros((2, CH, PAIRS, 2, CH), f)
    for qi in range(2):
        for qo in range(2):
            for k in range(PAIRS):
                tap = 2 * k + qi - qo
                if 0 <= tap < TAPS:
                    for g in range(CH // per):
                        s = slice(g * per, (g + 1) * per)
                        conv[qi, s, k, qo, s] = w[s, :, tap].T

    def by_parity(m):
        return m.reshape(HC // 2, P, 2, -1).transpose(1, 2, 0, 3).reshape(P, HC, -1)

    down = np.concatenate([by_parity(i["L1_ffn_lora_A"].transpose(1, 0, 2).reshape(H, E * R)),
                           by_parity(i["L1_ffn_gw1"].T)], axis=2)
    x = i["x"].reshape(N, H)
    return {
        "x": x,
        "x_t": x.reshape(NT, P, HC, P).transpose(0, 3, 2, 1).reshape(NT * P, H),
        "consts_a": a,
        "consts_b": b,
        "tok_ids": (np.arange(NT)[None, :] * P + np.arange(P)[:, None]).astype(np.int32),
        "zeros": np.zeros((P, E * N // P), np.int32),
        "expert_w": i["L0_ffn_expert_w"].reshape(E, HC, P, H),
        "conv_w": conv.reshape(P, PAIRS, P),
        "down_w": down,
        "main_w": by_parity(i["L1_ffn_weight"].T),
        "lora_b": i["L1_ffn_lora_B"].reshape(E * R, H),
    }


def kernel(**inputs):
    import concourse.bacc as bacc
    from concourse.bass_utils import run_bass_kernel_spmd

    nc = bacc.Bacc("TRN2", target_bir_lowering=False, num_devices=1)
    laid = lay_out({k: np.asarray(v) for k, v in inputs.items()})
    arrays, args = {}, []
    for name in INPUTS:
        a = np.ascontiguousarray(laid[name])
        arrays[f"in_{name}"] = a
        args.append(nc.dram_tensor(f"in_{name}", a.shape, mybir.dt.from_np(a.dtype), kind="ExternalInput").ap())
    out = nc.dram_tensor("out_0", (N, H), F32, kind="ExternalOutput").ap()
    build(nc, *args, out)
    r = run_bass_kernel_spmd(nc, [arrays], core_ids=[0])
    return r.results[0]["out_0"].reshape(B, CH, H)
```

```python
from contextlib import ExitStack

import numpy as np

import concourse.bass as bass
from concourse import mybir

ALU = mybir.AluOpType
ACT = mybir.ActivationFunctionType
AX = mybir.AxisListType
F32 = mybir.dt.float32
F32R = mybir.dt.float32r
I32 = mybir.dt.int32
U32 = mybir.dt.uint32

P = 128
B, CH, H = 32, 64, 1024
N = B * CH
NT = N // P
E = 8
K8 = 8
SLOTS = 2 * NT + E - 1
HC = H // P
HALF = H // 2
R = 16
HG = 4 * E
TAPS, PAD = 9, 4
PH = 4
CP = P // PH
CQ = CH // CP
WINS = (TAPS - 1 + PH - 1) // PH + 1
MW = (H + 2 * PAD) // PH
MC = H // PH // P
CAPACITY = int(3.0 * N / E)
ALPHA = 1.0 / R
TQ = NT * P // HALF
TG = NT // TQ
LN_EPS = 1e-5
CREDIT, DMA_CREDIT = 1, 16
G1W = E * R + HG


def columns(widths):
    at, out = 0, {}
    for name, w in widths:
        out[name] = (at, at + w)
        at += w
    return out, at


CA, CA_W = columns([("emb", B), ("w0", P), ("w1", P), ("w2", K8), ("b0", 1), ("b1", 1), ("b2", K8),
                    ("gate", HC * E), ("kern", K8 * CH), ("kbias", K8), ("ident", P), ("tri", P),
                    ("ones", P), ("iota", P), ("thr", NT - 1), ("cw", CH), ("fside", CH), ("tok", NT)])
CB, CB_W = columns([("gb1", HG), ("gamma", HG), ("beta", HG), ("gb2", E), ("gw2", E * HG)])


class Chain:

    def __init__(self, eng, sem, base=0):
        self.eng, self.sem, self.base, self.n = eng, sem, base, 0

    def add(self, ins):
        ins.then_inc(self.sem, 1)
        self.n += 1
        return self.n

    def wait(self, n=None):
        self.eng.wait_ge(self.sem, self.base + (self.n if n is None else n))

    def link(self, ins):
        self.add(ins)
        self.wait()


def build(nc, x, x_t, consts_a, consts_b, expert_w, conv_w, down_w, lora_b, out):
    ctx = ExitStack()
    with ctx:
        def sb(name, shape, dt=F32):
            return ctx.enter_context(nc.sbuf_tensor(name, shape, dt))

        def sem(name):
            return ctx.enter_context(nc.semaphore(name))

        def dram(name, shape, dt=F32):
            return nc.dram_tensor(name, shape, dt, kind="Internal").ap()

        c0_d = dram("c0_scratch", [N, H])
        y_d = dram("y_scratch", [(SLOTS + 1) * P, H])

        bank = [ctx.enter_context(nc.psum_tensor(f"bank{i}", [P, 512], F32)) for i in range(8)]

        ca = sb("ca", [P, CA_W])
        cb = sb("cb", [P, CB_W])
        conv_sb = sb("conv_sb", [P, WINS, CQ, P])
        down_sb = sb("down_sb", [P, HC, G1W])
        lora_sb = sb("lora_sb", [P, H])

        def c(name, rows=P):
            a, b = CA[name]
            return ca[0:rows, a:b]

        def d(name):
            a, b = CB[name]
            return cb[:, a:b]

        with nc.sbuf_tensor("weights_1", [P, 2, HC, H], F32R) as weights_1:
            pass
        res = sb("res", [P, NT, H])
        weights = [sb("weights_0", [P, 2, HC, H], F32R), weights_1]
        w_hi = [w[:, 0] for w in weights]
        w_lo = [w[:, 1] for w in weights]
        sel = res[:, NT - 4, 0:2 * NT * E].rearrange("p (t e) -> p t e", e=E)
        cmp = res[:, NT - 4, 2 * NT * E:2 * NT * E + E * (NT - 1)].rearrange("p (e t) -> p e t", e=E)
        prod = res[:, NT - 5, :].rearrange("p (k o) -> p k o", o=CH).rearrange("p (j k) o -> p j k o", j=2)
        aggb_t = res[:, NT - 3, 0:NT * K8].rearrange("p (t k) -> p t k", k=K8)
        l_hi = sb("l_hi", [P, HC, P], F32R)
        l_lo = sb("l_lo", [P, HC, P], F32R)
        work = sb("work", [P, 8 * H])

        def row(i, n=1):
            return work[:, i * H:(i + n) * H]

        x_sb = [row(0), row(1)]
        xt_sb = [row(2), row(3)]
        c0_sb = [row(4), row(5)]
        raw0 = row(6)
        oh_lo = row(7)[:, 0:4 * P].rearrange("p (m n) -> p m n", m=4)
        oh_hi = row(7)[:, 4 * P:8 * P].rearrange("p (m n) -> p m n", m=4)
        raw = [row(i) for i in range(4)]
        yo = row(6)
        xg = row(7)
        yg = [row(0, 2).rearrange("p (k n) -> p k n", k=2),
              row(2, 2).rearrange("p (k n) -> p k n", k=2)]
        c1 = row(4).rearrange("p (c m) -> p c m", c=HC)
        down_all = row(6, 2).rearrange("p (t n) -> p t n", t=NT)
        x1p = sb("x1p", [P, 2, CQ, MW])
        ctxb = sb("ctxb", [P, B, CH])

        h0 = sb("h0", [P, B])
        h1 = sb("h1", [P, B])
        at_l = sb("at_l", [B, K8])
        at_m = sb("at_m", [B, 1])
        at_n = sb("at_n", [B, 1])
        at_e = sb("at_e", [B, K8])
        at_s = sb("at_s", [B, 1])
        at_r = sb("at_r", [B, 1])
        att = sb("att", [B, K8])
        scratch = sb("scratch", [P, E * HG])
        attx = scratch[0:B, :].rearrange("p (n k) -> p n k", k=K8)
        attp = sb("attp", [P, NT * K8])
        gsum = sb("gsum", [P, E])
        aggb = sb("aggb", [P, NT])
        agg = sb("agg", [P, 2, CH])
        bd = [sb(f"bd{j}", [P, P]) for j in range(2)]
        g_sb = sb("g_sb", [P, 2 * E])
        lg = sb("lg", [P, 2, E])
        mx = sb("mx", [P, 2, 8])
        ix = sb("ix", [P, 2, 8], U32)
        mx_all = sb("mx_all", [P, NT, 2])
        ixf = sb("ixf", [P, 4])
        oh = sb("oh", [P, 2, 2, E])
        msk = sb("msk", [P, 2, E])
        pre = sb("pre", [P, 2, E])
        acc = sb("acc", [P, E])
        rk = sb("rk", [P, 2, 2, E])
        rk4 = sb("rk4", [P, 4])
        pos_s = sb("pos_s", [P, 4], I32)
        lo_i = sb("lo_i", [P, 4], I32)
        hi_i = sb("hi_i", [P, 4], I32)
        lo_f = sb("lo_f", [P, 4])
        hi_f = sb("hi_f", [P, 4])
        idx_all = sb("idx_all", [P, P], I32)
        rank_all = sb("rank_all", [P, 2 * NT])
        ix_all = sb("ix_all", [P, 2 * NT])
        base_f = sb("base_f", [P, 2 * NT])
        pos_all = sb("pos_all", [P, NT * 2], I32)
        tl = sb("tl", [P, E])
        cumf = sb("cumf", [P, E + 1])
        cum = sb("cum", [P, E + 1], I32)
        cnt = sb("cnt", [P, E + 1], I32)
        wd = sb("wd", [P, NT])
        we = sb("we", [P, NT])
        ws = sb("ws", [P, NT])
        w_all = sb("w_all", [P, NT, 2])
        idx = sb("idx", [P, 1], I32)
        ctx0 = sb("ctx0", [B, CH])
        ctxx = res[0:B, NT - 2:NT, :].rearrange("p t (n o) -> p (t n) o", o=CH)
        pos_c = [sb(f"pos_c{j}", [P, 2], I32) for j in range(2)]
        hb = sb("hb", [P, HG])
        st = sb("st", [P, 6])
        mv = sb("mv", [P, 2])
        ve = sb("ve", [P, 1])
        sd = sb("sd", [P, 1])
        rs = sb("rs", [P, 1])
        hn = sb("hn", [P, HG])
        hp = scratch[:, :].rearrange("p (e h) -> p e h", h=HG)
        gl = sb("gl", [P, E])
        gt = sb("gt", [P, E])
        mx2 = sb("mx2", [P, 8])
        ix2 = sb("ix2", [P, 8], U32)
        ixf2 = sb("ixf2", [P, 2])
        mx2_all = sb("mx2_all", [P, NT, 2])
        oh_all = row(5)[:, 4 * P:4 * P + 2 * NT * E].rearrange("p (t k e) -> p t k e", t=NT, k=2)
        acc2 = sb("acc2", [P, 2 * E])
        allow = sb("allow", [P, 2 * E])
        g2 = sb("g2", [P, NT, 2])
        w2_all = row(5)[:, 6 * P:6 * P + NT * E].rearrange("p (t e) -> p t e", e=E)
        up_hi, up_lo = w_hi[0][:, 0:2, 0:HALF], w_lo[0][:, 0:2, 0:HALF]
        twt_hi, twt_lo = w_hi[0][:, 2:2 + TQ, 0:HALF], w_lo[0][:, 2:2 + TQ, 0:HALF]

        s_apart = sem("s_apart")
        s_const = sem("s_const")
        s_x = [sem(f"s_x_{j}") for j in range(2)]
        s_xt = [sem(f"s_xt_{j}") for j in range(2)]
        s_raw0 = sem("s_raw0")
        s_raw = [sem(f"s_raw_{j}") for j in range(4)]
        s_hi = sem("s_hi")
        s_lo = sem("s_lo")
        s_late = sem("s_late")
        s_pe0 = sem("s_pe0")
        s_act0 = sem("s_act0")
        s_dve0 = sem("s_dve0")
        s_init = sem("s_init")
        s_attx = sem("s_attx")
        s_sm = sem("s_sm")
        s_agg = sem("s_agg")
        s_bd = [sem(f"s_bd_{j}") for j in range(2)]
        s_g = sem("s_g")
        s_gev = sem("s_gev")
        s_l = sem("s_l")
        s_lev = sem("s_lev")
        s_m = sem("s_m")
        s_r = sem("s_r")
        s_rev = sem("s_rev")
        s_c = [sem(f"s_c_{j}") for j in range(2)]
        s_cev = [sem(f"s_cev_{j}") for j in range(2)]
        s_cst = [sem(f"s_cst_{j}") for j in range(2)]
        s_pos = sem("s_pos")
        s_hot = sem("s_hot")
        s_list = sem("s_list")
        s_chA = sem("s_chA")
        s_cnt = sem("s_cnt")
        s_cum = sem("s_cum")
        s_chB = sem("s_chB")
        s_wd = sem("s_wd")
        s_we = sem("s_we")
        s_wall = sem("s_wall")
        s_cx = sem("s_cx")
        s_cxx = sem("s_cxx")
        s_cxb = sem("s_cxb")
        s_rest = sem("s_rest")
        s_idx = sem("s_idx")
        s_xg = sem("s_xg")
        s_ta = sem("s_ta")
        s_tb = sem("s_tb")
        s_ha = sem("s_ha")
        s_hb = sem("s_hb")
        s_la = sem("s_la")
        s_lb = sem("s_lb")
        s_fa = sem("s_fa")
        s_h0 = sem("s_h0")
        s_h1 = sem("s_h1")
        s_e0 = sem("s_e0")
        s_e1 = sem("s_e1")
        s_y0 = sem("s_y0")
        s_y1 = sem("s_y1")
        s_pad = sem("s_pad")
        s_pall = sem("s_pall")
        s_pc = sem("s_pc")
        s_yg = [sem(f"s_yg_{j}") for j in range(2)]
        s_xr = [sem(f"s_xr_{j}") for j in range(2)]
        s_chC = sem("s_chC")
        s_x1 = sem("s_x1")
        s_rel = sem("s_rel")
        s_cv = sem("s_cv")
        s_c1 = sem("s_c1")
        s_ch = sem("s_ch")
        s_cl = sem("s_cl")
        s_g1 = sem("s_g1")
        s_g1e = sem("s_g1e")
        s_ve = sem("s_ve")
        s_sd = sem("s_sd")
        s_m0 = sem("s_m0")
        s_m1 = sem("s_m1")
        s_me0 = sem("s_me0")
        s_me1 = sem("s_me1")
        s_a2 = sem("s_a2")
        s_t2 = sem("s_t2")
        s_chD = sem("s_chD")
        s_d2 = sem("s_d2")
        s_ex2 = sem("s_ex2")
        s_tw = sem("s_tw")
        s_twt = sem("s_twt")
        s_th = sem("s_th")
        s_tl = sem("s_tl")
        s_uh = sem("s_uh")
        s_ul = sem("s_ul")
        s_up = sem("s_up")
        s_fin = sem("s_fin")
        s_out = sem("s_out")

        tile_rows = lambda t: bass.ds(t * P, P)

        block = ctx.enter_context(nc.Block())

        def slots(eng, body):
            with eng.Fori(0, E // 2) as pair:
                for odd in range(2):
                    e = pair * 2 + odd
                    first = eng.value_load(cum[0:1, bass.ds(e, 1)], min_val=0, max_val=SLOTS)
                    count = eng.value_load(cnt[0:1, bass.ds(e, 1)], min_val=1, max_val=NT)
                    body(first, 0, e, odd, True)
                    with eng.Fori(1, count) as t:
                        body(first + t, t, e, odd, False)

        def wait_apart(eng, sem_, value):
            eng.wait_ge(sem_, value)
            eng.sem_inc(s_apart, 1)

        @block.sync
        def _(sp):
            for credited in (s_y0, s_y1, s_cst[0], s_cst[1]):
                sp.sem_inc(credited, DMA_CREDIT)
            for credited in (s_e0, s_e1, s_tb, s_g1e, s_me0, s_me1, s_a2):
                sp.sem_inc(credited, CREDIT)
            sp.dma_start(ca[:, :], consts_a).then_inc(s_const, 16)

            def load_x(rows, j):
                sp.dma_start(x_sb[j], x[rows, :]).then_inc(s_x[j], 16)

            def load_xt(rows, j):
                sp.dma_start(xt_sb[j], x_t[rows, :]).then_inc(s_xt[j], 16)

            def load_raw0(k):
                sp.dma_start(raw0, expert_w[0, k, :, :].rearrange("o p n -> p (o n)")).then_inc(s_raw0, 16)

            for j in range(2):
                load_xt(tile_rows(j), j)
            for j in range(2):
                load_x(tile_rows(j), j)
            load_raw0(bass.ds(0, 1))

            def phase_a(it, row0, nxt, last):
                if not last:
                    sp.wait_ge(s_g, it + 1)
                    for j in range(2):
                        load_xt(bass.ds(row0[j][1], P), j)
                for j in range(2):
                    if not last:
                        sp.wait_ge(s_c[j], it + 1)
                        load_x(bass.ds(row0[j][1], P), j)
                    sp.wait_ge(s_cev[j], 2 * (it + 1))
                    sp.dma_start(c0_d[bass.ds(row0[j][0], P), :], c0_sb[j]).then_inc(s_cst[j], 16)
                if not last:
                    sp.wait_ge(s_lo, it + 1)
                    load_raw0(nxt)

            with sp.Fori(0, NT // 2 - 1) as i:
                row0 = [[sp.snap((i * 2 + j + ahead) * P) for ahead in (0, 2)] for j in range(2)]
                nxt = bass.ds(sp.snap(i + 1), 1)
                phase_a(i, row0, nxt, False)
            it = NT // 2 - 1
            phase_a(it, [[(it * 2 + j) * P, 0] for j in range(2)], None, True)

            def load_raw(e, half):
                for k in range(HC // 2):
                    sp.dma_start(raw[k], expert_w[e, half * (HC // 2) + k, :, :].rearrange("o p n -> p (o n)")).then_inc(s_raw[k], 16)

            for j in range(2):
                sp.wait_ge(s_c[j], NT // 2)
            load_raw(bass.ds(1, 1), 0)
            for j in range(2):
                sp.wait_ge(s_cst[j], 16 * (NT // 2) + DMA_CREDIT)
            sp.wait_ge(s_cum, 1)

            def store0(g, rows):
                sp.wait_ge(s_e0, g + 1 + CREDIT)
                sp.dma_start(y_d[rows, 0:HALF], yo[:, 0:HALF]).then_inc(s_y0, 16)

            def store1(g, rows):
                sp.wait_ge(s_e1, g + 1 + CREDIT)
                sp.dma_start(y_d[rows, HALF:H], yo[:, HALF:H]).then_inc(s_y1, 16)

            def expert(e, last):
                first = sp.value_load(cum[0:1, bass.ds(e, 1)], min_val=0, max_val=SLOTS - 1)
                end = sp.value_load(cum[0:1, bass.ds(e + 1, 1)], min_val=1, max_val=SLOTS)
                second = sp.snap(first + 1)
                rows = bass.ds(sp.snap(first * P), P)
                nxt = bass.ds(sp.snap(e * 1 + 1), 1)
                nxt2 = None if last else bass.ds(sp.snap(e * 1 + 2), 1)
                sp.wait_ge(s_lo, (e + 1) * HC + HC // 2)
                load_raw(nxt, 1)
                store0(first, rows)
                store1(first, rows)
                if not last:
                    sp.wait_ge(s_lo, (e + 1) * HC + HC)
                    load_raw(nxt2, 0)
                with sp.Fori(second, end) as g:
                    rows = bass.ds(sp.snap(g * P), P)
                    store0(g, rows)
                    store1(g, rows)

            with sp.Fori(0, 1) as e:
                expert(e, False)
            with sp.Fori(sp.value_load(cum[0:1, E:E + 1], min_val=E, max_val=SLOTS), SLOTS + 1) as g:
                sp.dma_start(y_d[bass.ds(sp.snap(g * P), P), :], c0_sb[0]).then_inc(s_rest, 16)
            sp.dma_start(cb[:, :], consts_b).then_inc(s_late, 16)
            sp.dma_start(conv_sb[:, :, :, :], conv_w).then_inc(s_late, 16)
            sp.dma_start(down_sb[:, :, :], down_w).then_inc(s_late, 16)
            sp.dma_start(lora_sb[:, :], lora_b).then_inc(s_late, 16)
            with sp.Fori(1, E - 1) as e:
                expert(e, False)
            with sp.Fori(E - 1, E) as e:
                expert(e, True)

            total = sp.value_load(cum[0:1, E:E + 1], min_val=E, max_val=SLOTS)
            unused = sp.value_load(cnt[0:1, E:E + 1], min_val=1, max_val=SLOTS + 1)
            wait_apart(sp, s_rest, unused * 16)
            sp.wait_ge(s_h1, total)

            def load_res(t, at, j):
                sp.dma_start(res[:, bass.ds(at, 1), :].rearrange("p o n -> p (o n)"), x[bass.ds(t, P), :]).then_inc(s_xr[j], 16)

            for j in range(2):
                load_res(j * P, j, j)
            with sp.Fori(1, NT // 2) as i:
                at = [[sp.snap((i * 2 + j) * P), sp.snap(i * 2 + j)] for j in range(2)]
                for j in range(2):
                    sp.wait_ge(s_xr[j], i * 16)
                    load_res(at[j][0], at[j][1], j)
            with sp.Fori(0, NT) as t:
                rows = bass.ds(sp.snap(t * P), P)
                at = sp.snap(t * 1)
                sp.wait_ge(s_fin, (t + 1) * 2)
                sp.dma_start(out[rows, :], res[:, bass.ds(at, 1), :].rearrange("p o n -> p (o n)")).then_inc(s_out, 16)
            sp.wait_ge(s_out, 16 * NT)

        @block.gpsimd
        def _(pool):
            for j in range(2):
                pool.memset(bd[j][:, :], 0.0).then_inc(s_init, 1)
            for a in (0, MW - 1):
                pool.memset(x1p[:, :, :, a:a + 1], 0.0).then_inc(s_pad, 1)
            pool.memset(acc[:, :], 0.0).then_inc(s_init, 1)
            pool.memset(acc2[:, :], 0.0).then_inc(s_init, 1)
            pool.memset(cumf[:, 0:1], 0.0).then_inc(s_init, 1)

            def rest0(it):
                wait_apart(pool, s_hi, it + 1)
                at = bass.ds(it, 1)
                pool.tensor_tensor(w_lo[0][:, at, :].rearrange("p o n -> p (o n)"), raw0,
                                   w_hi[0][:, at, :].rearrange("p o n -> p (o n)").bitcast(F32), ALU.subtract).then_inc(s_lo, 1)

            with pool.Fori(0, NT // 2) as it:
                rest0(it)
            pool.wait_ge(s_cum, 1)
            for j in range(2):
                pool.wait_ge(s_cst[j], 16 * (NT // 2) + DMA_CREDIT)

            def gather():
                pool.indirect_dma_start(xg, None, c0_d, bass.IndirectOffsetOnAxis(ap=idx[:, 0:1], axis=0)).then_inc(s_xg, 16)

            def slot(g, t, e, odd, first):
                pool.tensor_copy(idx[:, :], idx_all[:, bass.ds(pool.snap(e * NT + t), 1)]).then_inc(s_idx, 1)
                wait_apart(pool, s_idx, g + 1)
                wait_apart(pool, s_tb, g + CREDIT)
                gather()
                wait_apart(pool, s_xg, (g + 1) * 16)

            slots(pool, slot)
            total = pool.value_load(cum[0:1, E:E + 1], min_val=E, max_val=SLOTS)
            wait_apart(pool, s_tb, total + CREDIT)
            gather()
            pool.wait_ge(s_pall, 1)
            pool.wait_ge(s_lo, (E + 1) * HC)
            wait_apart(pool, s_y0, total * 16 + DMA_CREDIT)
            wait_apart(pool, s_y1, total * 16 + DMA_CREDIT)

            def fetch(t, j, it):
                pool.tensor_copy(pos_c[j][:, :], pos_all[:, bass.ds(t * 2, 2)]).then_inc(s_pc, 1)
                wait_apart(pool, s_pc, t + 1)
                for k in range(2):
                    pool.indirect_dma_start(yg[j][:, k, :], None, y_d,
                                            bass.IndirectOffsetOnAxis(ap=pos_c[j][:, k:k + 1], axis=0)).then_inc(s_yg[j], 16)

            fetch(0, 0, 0)
            fetch(1, 1, 0)
            with pool.Fori(1, NT // 2) as i:
                for j in range(2):
                    wait_apart(pool, s_x1, i * 2 + j - 1)
                    fetch(i * 2 + j, j, i)

        @block.scalar
        def _(act):
            act.wait_ge(s_const, 16)
            act.wait_ge(s_pe0, 1)
            act.activation(h0[:, :], bank[0][:, 0:B], ACT.Gelu, bias=c("b0")).then_inc(s_act0, 1)
            act.wait_ge(s_pe0, 4)
            act.activation(h1[:, :], bank[1][:, 0:B], ACT.Gelu, bias=c("b1")).then_inc(s_act0, 1)
            act.wait_ge(s_sm, 1)
            act.activation(at_e[:, :], at_l[:, :], ACT.Exp, bias=at_n[:, :], accum_out=at_s[:, :]).then_inc(s_act0, 1)

            def spread(j, it):
                act.wait_ge(s_agg, it + 1)
                act.activation(bd[j][0:CH, 0:CH], agg[0:CH, j, :], ACT.Copy).then_inc(s_bd[j], 1)
                act.activation(bd[j][CH:P, CH:P], agg[CH:P, j, :], ACT.Copy).then_inc(s_bd[j], 1)

            act.wait_ge(s_init, 5)
            for j in range(2):
                spread(j, 0)

            def phase_a(it, last):
                act.wait_ge(s_raw0, (it + 1) * 16)
                act.activation(w_hi[0][:, bass.ds(it, 1), :].rearrange("p o n -> p (o n)"), raw0, ACT.Copy).then_inc(s_hi, 1)
                for j in range(2):
                    act.wait_ge(s_c[j], it + 1)
                    if not last:
                        spread(j, it + 1)
                    act.wait_ge(s_cst[j], it * 16 + DMA_CREDIT)
                    for h in range(2):
                        act.activation(c0_sb[j][:, h * HALF:(h + 1) * HALF], bank[2 * j + h][:, :], ACT.Identity,
                                       bias=aggb[:, bass.ds(it * 2 + j, 1)]).then_inc(s_cev[j], 1)

            with act.Fori(0, NT // 2 - 1) as it:
                phase_a(it, False)
            phase_a(NT // 2 - 1, True)

            def round_a(g):
                act.wait_ge(s_ta, g + 1)
                act.wait_ge(s_fa, g)
                act.activation(l_hi[:, 0:4, :], bank[2][:, :].rearrange("p (c m) -> p c m", c=4), ACT.Copy).then_inc(s_ha, 1)

            def round_b(g):
                act.wait_ge(s_tb, g + 1 + CREDIT)
                act.wait_ge(s_h1, g)
                act.activation(l_hi[:, 4:8, :], bank[3][:, :].rearrange("p (c m) -> p c m", c=4), ACT.Copy).then_inc(s_hb, 1)

            def round_w(e, odd, half):
                for k in range(HC // 2):
                    act.wait_ge(s_raw[k], e * 32 + (half + 1) * 16)
                    act.activation(w_hi[1 - odd][:, half * (HC // 2) + k, :], raw[k], ACT.Copy).then_inc(s_hi, 1)

            round_a(0)
            round_b(0)
            act.wait_ge(s_wd, 1)
            act.activation(we[:, :], wd[:, :], ACT.Exp).then_inc(s_we, 1)
            act.wait_ge(s_cum, 1)

            def slot(g, t, e, odd, first):
                if first:
                    round_w(e, odd, 0)
                act.wait_ge(s_h0, g + 1)
                act.wait_ge(s_y0, g * 16 + DMA_CREDIT)
                act.activation(yo[:, 0:HALF], bank[0][:, :], ACT.Copy).then_inc(s_e0, 1)
                round_a(g + 1)
                round_b(g + 1)
                act.wait_ge(s_y1, g * 16 + DMA_CREDIT)
                act.activation(yo[:, HALF:H], bank[1][:, :], ACT.Copy).then_inc(s_e1, 1)
                if first:
                    round_w(e, odd, 1)

            slots(act, slot)

            act.wait_ge(s_pad, 2)

            def rearrange(t, free, parts=(0, 1)):
                act.wait_ge(s_x1, t + 1)
                if free is not None:
                    act.wait_ge(s_cv, free)
                for b in parts:
                    for u in range(CQ):
                        a = b * CH + u * CP
                        rows = res[a:a + CP, bass.ds(t, 1), :].rearrange("p o (m q) -> p (o m) q", q=PH)
                        for q in range(PH):
                            act.activation(x1p[q * CP:(q + 1) * CP, b, u, 1:MW - 1], rows[:, :, q], ACT.Copy).then_inc(s_rel, 1)

            def round_c(t):
                act.wait_ge(s_c1, (t + 1) * 2)
                act.wait_ge(s_m1, t)
                for h in range(2):
                    act.activation(l_hi[:, h * 4:(h + 1) * 4, :], c1[:, h * 4:(h + 1) * 4, :], ACT.Copy).then_inc(s_ch, 1)

            def root(t):
                act.wait_ge(s_ve, t + 1)
                act.activation(sd[:, :], ve[:, :], ACT.Sqrt).then_inc(s_sd, 1)

            rearrange(0, None, (0,))
            rearrange(1, 2)
            round_c(0)
            root(0)
            rearrange(2, 4)
            with act.Fori(1, NT - 2) as t:
                round_c(t)
                root(t)
                rearrange(t + 2, (t + 2) * 2)
            for t in range(NT - 2, NT):
                round_c(t)
                root(t)
            act.wait_ge(s_d2, 1)
            act.activation(we[:, :], wd[:, :], ACT.Exp).then_inc(s_ex2, 1)
            act.wait_ge(s_m0, NT)
            for h in range(2):
                act.activation(up_hi[:, h, :], lora_sb[:, h * HALF:(h + 1) * HALF], ACT.Copy).then_inc(s_uh, 1)
            for q in range(TQ):
                act.wait_ge(s_twt, q + 1)
                act.activation(twt_hi[:, q, :], bank[4 + q][:, :], ACT.Copy).then_inc(s_th, 1)

        @block.vector
        def _(dve):
            ch = Chain(dve, s_dve0)
            dve.wait_ge(s_const, 16)
            dve.wait_ge(s_pe0, 2)
            ch.add(dve.tensor_copy(gsum[:, :], bank[2][:, 0:E]))
            dve.wait_ge(s_pe0, 3)
            ch.link(dve.tensor_copy(ctx0[:, :], bank[3][0:B, 0:CH]))
            dve.wait_ge(s_pe0, 5)
            ch.link(dve.tensor_tensor(at_l[:, :], bank[4][0:B, 0:K8], c("b2", B), ALU.add))
            ch.link(dve.tensor_reduce(at_m[:, :], at_l[:, :], AX.X, ALU.max))
            dve.tensor_scalar(at_n[:, :], at_m[:, :], -1.0, None, ALU.mult).then_inc(s_sm, 1)
            dve.wait_ge(s_act0, 3)
            ch.link(dve.reciprocal(at_r[:, :], at_s[:, :]))
            ch.link(dve.tensor_scalar(att[:, :], at_e[:, :], at_r[:, 0:1], None, ALU.mult))
            dve.tensor_tensor(attx[:, :, :], c("ident", B)[:, 0:B].unsqueeze(2).to_broadcast([B, B, K8]),
                              att[:, :].unsqueeze(1).to_broadcast([B, B, K8]), ALU.mult).then_inc(s_attx, 1)
            dve.wait_ge(s_pe0, 6)
            spread = bank[5][:, 0:B * K8].rearrange("p (t q k) -> p t q k", q=2, k=K8)
            attp3 = attp[:, :].rearrange("p (t k) -> p t k", k=K8)
            for q in range(2):
                ch.add(dve.tensor_copy(attp3[q * CH:(q + 1) * CH, :, :], spread[q * CH:(q + 1) * CH, :, q, :]))
            ch.wait()
            ch.link(dve.tensor_tensor(aggb_t[:, :, :], attp3, c("kbias").unsqueeze(1).to_broadcast([P, NT, K8]), ALU.mult))
            ch.link(dve.tensor_reduce(aggb[:, :], aggb_t[:, :, :], AX.X, ALU.add))

            kern = c("kern").rearrange("p (k o) -> p k o", k=K8)

            def aggregate(ch, it, free):
                if free is not None:
                    for j in range(2):
                        dve.wait_ge(s_bd[j], free)
                w = attp[:, bass.ds(it * 2 * K8, 2 * K8)].rearrange("p (j k) -> p j k", j=2)
                ch.link(dve.tensor_tensor(prod, kern.unsqueeze(1).to_broadcast([P, 2, K8, CH]),
                                          w.unsqueeze(3).to_broadcast([P, 2, K8, CH]), ALU.mult))
                dve.tensor_reduce(agg[:, :, :], prod.rearrange("p j k o -> p j o k"), AX.X, ALU.add).then_inc(s_agg, 1)

            aggregate(ch, 0, None)

            oh4 = oh[:, :, :, :].rearrange("p j k e -> p (j k) e")
            rk4v = rk[:, :, :, :].rearrange("p j k e -> p (j k) e")
            iota4 = c("iota")[:, 0:E].unsqueeze(1).to_broadcast([P, 4, E])

            def take_gate(it):
                dve.wait_ge(s_g, it + 1)
                dve.wait_ge(s_l, it)
                dve.tensor_copy(g_sb[:, :], bank[4][:, 0:2 * E]).then_inc(s_gev, 1)

            def place(ch, it, first=False):
                dve.wait_ge(s_r, it + 1)
                ranks = bank[6][:, 0:2 * E].rearrange("p (j e) -> p j e", j=2)
                for k in range(2):
                    n = ch.add(dve.tensor_tensor(rk[:, :, k, :], oh[:, :, k, :], ranks, ALU.mult))
                ch.wait(n)
                ch.link(dve.tensor_reduce(rk4[:, :], rk4v, AX.X, ALU.add))
                ch.add(dve.tensor_copy(rank_all[:, bass.ds(it * 4, 4)], rk4[:, :]))
                ch.add(dve.tensor_copy(ix_all[:, bass.ds(it * 4, 4)], ixf[:, :]))
                ch.link(dve.scalar_tensor_tensor(pos_s[:, :], ixf[:, :], float(N), rk4[:, :], ALU.mult, ALU.add))
                ch.add(dve.tensor_scalar(lo_i[:, :], pos_s[:, :], P - 1, None, ALU.bitwise_and))
                ch.link(dve.tensor_scalar(hi_i[:, :], pos_s[:, :], P.bit_length() - 1, None, ALU.arith_shift_right))
                ch.add(dve.tensor_copy(lo_f[:, :], lo_i[:, :]))
                ch.link(dve.tensor_copy(hi_f[:, :], hi_i[:, :]))
                one_hot(it, first)

            def one_hot(it, first):
                if not first:
                    dve.wait_ge(s_list, it)
                for m in range(4):
                    dve.tensor_scalar(oh_lo[:, m, :], c("iota"), lo_f[:, m:m + 1], None, ALU.is_equal)
                    ins = dve.tensor_scalar(oh_hi[:, m, :], c("iota"), hi_f[:, m:m + 1],
                                            c("tok")[:, bass.ds(it * 2 + m // 2, 1)], ALU.is_equal, ALU.mult)
                ins.then_inc(s_hot, 1)

            def route(ch, it):
                dve.wait_ge(s_l, it + 1)
                for j in range(2):
                    n = ch.add(dve.scalar_tensor_tensor(lg[:, j, :], gsum[:, :], aggb[:, bass.ds(it * 2 + j, 1)],
                                                        bank[5][:, j * E:(j + 1) * E], ALU.mult, ALU.add))
                wait_apart(dve, s_chA, ch.base + n)
                for j in range(2):
                    n = ch.add(dve.max(mx[:, j, :], lg[:, j, :]))
                ch.wait(n)
                ch.add(dve.tensor_copy(mx_all[:, bass.ds(it * 2, 2), :], mx[:, :, 0:2]))
                for j in range(2):
                    ch.add(dve.max_index(ix[:, j, :], mx[:, j, :], lg[:, j, :]))
                ch.wait()
                ch.link(dve.tensor_copy(ixf[:, :].rearrange("p (j k) -> p j k", j=2), ix[:, :, 0:2]))
                ch.link(dve.tensor_tensor(oh4, iota4, ixf[:, :].unsqueeze(2).to_broadcast([P, 4, E]), ALU.is_equal))
                dve.wait_ge(s_m, it)
                ch.add(dve.tensor_copy(pre[:, 0, :], acc[:, :]))
                ch.link(dve.tensor_tensor(msk[:, :, :], oh[:, :, 0, :], oh[:, :, 1, :], ALU.add))
                ch.link(dve.tensor_tensor(pre[:, 1, :], pre[:, 0, :], msk[:, 0, :], ALU.add))
                dve.tensor_tensor(acc[:, :], pre[:, 1, :], msk[:, 1, :], ALU.add).then_inc(s_m, 1)

            LA = 23
            dve.wait_ge(s_init, 5)
            take_gate(0)
            ca0 = Chain(dve, s_chA)
            route(ca0, 0)
            aggregate(ca0, 1, 2)
            take_gate(1)
            place(ca0, 0, True)
            route(ca0, 1)
            aggregate(ca0, 2, 4)
            base = ca0.n
            with dve.Fori(2, NT // 2 - 1) as it:
                ch = Chain(dve, s_chA, (it - 2) * LA + base)
                take_gate(it)
                place(ch, it - 1)
                route(ch, it)
                aggregate(ch, it + 1, (it + 1) * 2)
                assert ch.n == LA, ch.n
            ch = Chain(dve, s_chA, base + LA * (NT // 2 - 3))
            it = NT // 2 - 1
            take_gate(it)
            place(ch, it - 1)
            route(ch, it)
            place(ch, it)
            dve.wait_ge(s_list, NT // 2)
            dve.tensor_copy(idx_all[:, :], bank[7][:, 0:P])

            ch = Chain(dve, s_chB)
            dve.wait_ge(s_cnt, 1)
            ch.link(dve.tensor_tensor(cmp[:, :, :], bank[4][:, 0:E].unsqueeze(2).to_broadcast([P, E, NT - 1]),
                                      c("thr").unsqueeze(1).to_broadcast([P, E, NT - 1]), ALU.is_gt))
            ch.link(dve.tensor_reduce(tl[:, :], cmp[:, :, :], AX.X, ALU.add))
            for e in range(E):
                ch.link(dve.scalar_tensor_tensor(cumf[:, e + 1:e + 2], tl[:, e:e + 1], 1.0, cumf[:, e:e + 1], ALU.add, ALU.add))
            ch.add(dve.tensor_scalar(cnt[:, 0:E], tl[:, :], 1.0, None, ALU.add))
            ch.link(dve.tensor_scalar(cnt[:, E:E + 1], cumf[:, E:E + 1], -1.0, float(SLOTS + 1), ALU.mult, ALU.add))
            dve.tensor_copy(cum[:, :], cumf[:, :]).then_inc(s_cum, 1)

            def rest_a(g):
                dve.wait_ge(s_ha, g + 1)
                dve.tensor_tensor(l_lo[:, 0:4, :], bank[2][:, :].rearrange("p (c m) -> p c m", c=4),
                                  l_hi[:, 0:4, :].bitcast(F32), ALU.subtract).then_inc(s_la, 1)

            def rest_b(g):
                dve.wait_ge(s_hb, g + 1)
                dve.tensor_tensor(l_lo[:, 4:8, :], bank[3][:, :].rearrange("p (c m) -> p c m", c=4),
                                  l_hi[:, 4:8, :].bitcast(F32), ALU.subtract).then_inc(s_lb, 1)

            dve.tensor_tensor(ctxx[:, :, :], c("ident", B)[:, 0:B].unsqueeze(2).to_broadcast([B, B, CH]),
                              ctx0[:, :].unsqueeze(1).to_broadcast([B, B, CH]), ALU.mult).then_inc(s_cxx, 1)
            rest_a(0)
            rest_b(0)
            dve.tensor_tensor(wd[:, :], mx_all[:, :, 1], mx_all[:, :, 0], ALU.subtract).then_inc(s_wd, 1)
            dve.wait_ge(s_we, 1)
            ch.link(dve.tensor_scalar(ws[:, :], we[:, :], 1.0, None, ALU.add))
            ch.link(dve.reciprocal(w_all[:, :, 0], ws[:, :]))
            ch.link(dve.tensor_tensor(w_all[:, :, 1], we[:, :], w_all[:, :, 0], ALU.mult))
            dve.wait_ge(s_cxb, 1)
            ctx4 = ctxb[:, :, :].rearrange("p (q n) o -> p q n o", q=4)
            for q in range(4):
                dve.tensor_tensor(ctx4[:, q], bank[4 + q][:, :].rearrange("p (n o) -> p n o", o=CH),
                                  c("fside").unsqueeze(1).to_broadcast([P, B // 4, CH]), ALU.add).then_inc(s_cx, 1)
            ch.link(dve.tensor_tensor(sel[:, :, :], c("iota")[:, 0:E].unsqueeze(1).to_broadcast([P, 2 * NT, E]),
                                      ix_all[:, :].unsqueeze(2).to_broadcast([P, 2 * NT, E]), ALU.is_equal))
            ch.link(dve.tensor_tensor(sel[:, :, :], sel[:, :, :],
                                      cumf[:, 0:E].unsqueeze(1).to_broadcast([P, 2 * NT, E]), ALU.mult))
            ch.link(dve.tensor_reduce(base_f[:, :], sel[:, :, :], AX.X, ALU.add))
            dve.scalar_tensor_tensor(pos_all[:, :], base_f[:, :], float(P), rank_all[:, :], ALU.mult, ALU.add).then_inc(s_pall, 1)

            def rest_w(e, odd, half):
                for k in range(HC // 2):
                    at = half * (HC // 2) + k
                    dve.wait_ge(s_hi, e * HC + (HC + at + 1))
                    dve.tensor_tensor(w_lo[1 - odd][:, at, :], raw[k], w_hi[1 - odd][:, at, :].bitcast(F32),
                                      ALU.subtract).then_inc(s_lo, 1)

            def slot(g, t, e, odd, first):
                if first:
                    rest_w(e, odd, 0)
                rest_a(g + 1)
                rest_b(g + 1)
                if first:
                    rest_w(e, odd, 1)

            dve.wait_ge(s_lo, HC)
            slots(dve, slot)

            dve.wait_ge(s_late, 64)
            dve.wait_ge(s_cx, 4)

            LC = 15
            def combine(ch, t, j, it):
                dve.wait_ge(s_yg[j], (it + 1) * 32)
                dve.wait_ge(s_xr[j], (it + 1) * 16)
                rows = res[:, bass.ds(t, 1), :].rearrange("p o n -> p (o n)")
                w2 = w_all[:, bass.ds(t, 1), :].rearrange("p o k -> p (o k)")
                ch.link(dve.scalar_tensor_tensor(rows, yg[j][:, 0, :], w2[:, 0:1], rows, ALU.mult, ALU.add))
                dve.scalar_tensor_tensor(rows, yg[j][:, 1, :], w2[:, 1:2], rows, ALU.mult, ALU.add).then_inc(s_x1, 1)

            def take_conv(t):
                out4 = c1.rearrange("p k (b u o) -> p b u k o", b=2, u=CQ)
                for b in range(2):
                    dve.wait_ge(s_cv, t * 2 + b + 1)
                    if b == 0 and not isinstance(t, int):
                        dve.wait_ge(s_cl, t * 2)
                    add = ctxb[:, bass.ds(t * 2 + b, 1), :].rearrange("p n (u o) -> p (n u) o", u=CQ)
                    ps = bank[4 + b][:, :].rearrange("p (u k o) -> p u k o", u=CQ, k=HC)
                    dve.tensor_tensor(out4[:, b], ps, add.unsqueeze(2).to_broadcast([P, CQ, HC, CP]), ALU.add).then_inc(s_c1, 1)

            def rest_c(t):
                for h in range(2):
                    dve.wait_ge(s_ch, t * 2 + h + 1)
                    dve.tensor_tensor(l_lo[:, h * 4:(h + 1) * 4, :], c1[:, h * 4:(h + 1) * 4, :],
                                      l_hi[:, h * 4:(h + 1) * 4, :].bitcast(F32), ALU.subtract).then_inc(s_cl, 1)

            def gate(ch, t):
                dve.wait_ge(s_g1, t + 1)
                down = down_all[:, bass.ds(t, 1), :].rearrange("p o n -> p (o n)")
                dve.tensor_copy(down, bank[2][:, 0:E * R])
                dve.tensor_tensor(hb[:, :], bank[2][:, E * R:G1W], d("gb1"), ALU.add).then_inc(s_g1e, 1)
                wait_apart(dve, s_g1e, t + 1 + CREDIT)
                ch.add(dve.bn_stats(st[:, :], hb[:, :]))
                wait_apart(dve, s_chC, ch.base + ch.n)
                ch.link(dve.bn_aggr(mv[:, :], st[:, :]))
                dve.tensor_scalar(ve[:, :], mv[:, 1:2], LN_EPS, None, ALU.add).then_inc(s_ve, 1)
                dve.wait_ge(s_sd, t + 1)
                ch.link(dve.reciprocal(rs[:, :], sd[:, :]))
                ch.link(dve.tensor_scalar(hn[:, :], hb[:, :], mv[:, 0:1], rs[:, 0:1], ALU.subtract, ALU.mult))
                ch.link(dve.tensor_tensor(hb[:, :], hn[:, :], d("gamma"), ALU.mult))
                ch.link(dve.tensor_tensor(hn[:, :], hb[:, :], d("beta"), ALU.add))
                ch.link(dve.scalar_tensor_tensor(hp[:, :, :], hn[:, :].unsqueeze(1).to_broadcast([P, E, HG]), 0.0,
                                                 d("gw2").rearrange("p (e h) -> p e h", e=E), ALU.max, ALU.mult))
                ch.link(dve.tensor_reduce(gl[:, :], hp[:, :, :], AX.X, ALU.add))
                ch.add(dve.tensor_tensor(gt[:, :], gl[:, :], d("gb2"), ALU.add))
                wait_apart(dve, s_chC, ch.base + ch.n)
                ch.link(dve.max(mx2[:, :], gt[:, :]))
                ch.add(dve.tensor_copy(mx2_all[:, bass.ds(t, 1), :].rearrange("p o k -> p (o k)"), mx2[:, 0:2]))
                ch.link(dve.max_index(ix2[:, :], mx2[:, :], gt[:, :]))
                ch.link(dve.tensor_copy(ixf2[:, :], ix2[:, 0:2]))
                ohv = oh_all[:, bass.ds(t, 1), :, :].rearrange("p o k e -> p (o k) e")
                ch.link(dve.tensor_tensor(ohv, c("iota")[:, 0:E].unsqueeze(1).to_broadcast([P, 2, E]),
                                          ixf2[:, :].unsqueeze(2).to_broadcast([P, 2, E]), ALU.is_equal))
                acc2v = acc2[:, :].rearrange("p (k e) -> p k e", k=2)
                dve.wait_ge(s_a2, t + CREDIT)
                dve.tensor_tensor(acc2v, acc2v, ohv, ALU.add).then_inc(s_a2, 1)

            def take_main(t):
                rows = res[:, bass.ds(t, 1), :].rearrange("p o n -> p (o n)")
                for h, (s, done) in enumerate(((s_m0, s_me0), (s_m1, s_me1))):
                    dve.wait_ge(s, t + 1)
                    half = rows[:, h * HALF:(h + 1) * HALF]
                    dve.tensor_tensor(half, bank[h][:, :], half, ALU.add).then_inc(done, 1)

            ch = Chain(dve, s_chC)
            combine(ch, 0, 0, 0)
            dve.wait_ge(s_pad, 2)
            dve.wait_ge(s_x1, 1)
            for u in range(CQ):
                a = CH + u * CP
                for q in range(PH):
                    dve.tensor_copy(x1p[q * CP:(q + 1) * CP, 1, u, 1:MW - 1],
                                    res[a:a + CP, 0, :].rearrange("p (m q) -> p m q", q=PH)[:, :, q]).then_inc(s_rel, 1)
            combine(ch, 1, 1, 0)
            take_conv(0)
            with dve.Fori(0, NT // 2 - 1) as i:
                ch = Chain(dve, s_chC, i * (2 * LC) + 2)
                for j in range(2):
                    t = i * 2 + j
                    rest_c(t)
                    combine(ch, t + 2, j, i + 1)
                    gate(ch, t)
                    take_conv(t + 1)
                    take_main(t)
                assert ch.n == 2 * LC, ch.n
            ch = Chain(dve, s_chC, (NT // 2 - 1) * 2 * LC + 2)
            rest_c(NT - 2)
            gate(ch, NT - 2)
            take_conv(NT - 1)
            take_main(NT - 2)
            rest_c(NT - 1)
            gate(ch, NT - 1)

            ch = Chain(dve, s_chD)
            dve.tensor_tensor(wd[:, :], mx2_all[:, :, 1], mx2_all[:, :, 0], ALU.subtract).then_inc(s_d2, 1)
            dve.wait_ge(s_ex2, 1)
            ch.link(dve.tensor_scalar(ws[:, :], we[:, :], 1.0, None, ALU.add))
            ch.link(dve.reciprocal(g2[:, :, 0], ws[:, :]))
            ch.link(dve.tensor_tensor(g2[:, :, 1], we[:, :], g2[:, :, 0], ALU.mult))
            dve.wait_ge(s_t2, 1)
            ch.link(dve.tensor_scalar(allow[:, :], bank[2][:, 0:2 * E], float(CAPACITY), None, ALU.is_le))
            oh_t = oh_all[:, :, :, :].rearrange("p t k e -> p t (k e)")
            oh_k = oh_all[:, :, :, :].rearrange("p t k e -> p (t k) e")
            ch.link(dve.tensor_tensor(oh_t, oh_t, allow[:, :].unsqueeze(1).to_broadcast([P, NT, 2 * E]), ALU.mult))
            g2v = g2[:, :, :].rearrange("p t k -> p (t k)").unsqueeze(2).to_broadcast([P, 2 * NT, E])
            ch.link(dve.tensor_tensor(oh_k, oh_k, g2v, ALU.mult))
            ch.link(dve.tensor_tensor(w2_all[:, :, :], oh_all[:, :, 0, :], oh_all[:, :, 1, :], ALU.add))

            for q in range(TQ):
                rows = down_all[:, q * TG:(q + 1) * TG, :].rearrange("p t (e r) -> p (t e) r", r=R)
                w = w2_all[:, q * TG:(q + 1) * TG, :].rearrange("p t e -> p (t e)").unsqueeze(2).to_broadcast([P, TG * E, R])
                dve.scalar_tensor_tensor(rows, rows, ALPHA, w, ALU.mult, ALU.mult).then_inc(s_tw, 1)
            for h in range(2):
                dve.wait_ge(s_uh, h + 1)
                dve.tensor_tensor(up_lo[:, h, :], lora_sb[:, h * HALF:(h + 1) * HALF], up_hi[:, h, :].bitcast(F32),
                                  ALU.subtract).then_inc(s_ul, 1)
            take_main(NT - 1)
            for q in range(TQ):
                dve.wait_ge(s_th, q + 1)
                dve.tensor_tensor(twt_lo[:, q, :], bank[4 + q][:, :], twt_hi[:, q, :].bitcast(F32),
                                  ALU.subtract).then_inc(s_tl, 1)
            with dve.Fori(0, NT // 2) as i:
                for j in range(2):
                    t = i * 2 + j
                    rows = res[:, bass.ds(t, 1), :].rearrange("p o n -> p (o n)")
                    for h in range(2):
                        dve.wait_ge(s_up, t * 2 + h + 1)
                        half = rows[:, h * HALF:(h + 1) * HALF]
                        dve.tensor_tensor(half, bank[2 * (1 - j) + h][:, :], half, ALU.add).then_inc(s_fin, 1)

        @block.tensor
        def _(pe):
            ones = c("ones")
            ident = c("ident")
            gatec = c("gate").rearrange("p (c e) -> p c e", c=HC)
            pe.wait_ge(s_const, 16)
            pe.matmul(bank[0][:, 0:B], c("w0"), c("emb"), start=True, stop=True).then_inc(s_pe0, 1)
            for k in range(HC):
                mm = pe.matmul(bank[2][:, 0:E], ones, gatec[:, k, :], start=(k == 0), stop=(k == HC - 1))
            mm.then_inc(s_pe0, 1)
            pe.matmul(bank[3][0:B, 0:CH], c("emb"), c("cw"), start=True, stop=True).then_inc(s_pe0, 1)
            pe.wait_ge(s_act0, 1)
            pe.matmul(bank[1][:, 0:B], c("w1"), h0[:, :], start=True, stop=True).then_inc(s_pe0, 1)
            pe.wait_ge(s_act0, 2)
            pe.matmul(bank[4][0:B, 0:K8], h1[:, :], c("w2"), start=True, stop=True).then_inc(s_pe0, 1)
            pe.wait_ge(s_attx, 1)
            pe.matmul(bank[5][:, 0:B * K8], c("ones", B), attx[:, :, :].rearrange("p n k -> p (n k)"),
                      start=True, stop=True).then_inc(s_pe0, 1)
            pe.wait_ge(s_agg, 1)

            def ranks(it):
                pe.wait_ge(s_m, it + 1)
                pe.matmul(bank[6][:, 0:2 * E], c("tri"), msk[:, :, :].rearrange("p j e -> p (j e)"), start=True, stop=False)
                pe.matmul(bank[6][:, 0:2 * E], ones, pre[:, :, :].rearrange("p j e -> p (j e)"),
                          start=False, stop=True).then_inc(s_r, 1)

            def lists(it, first, last):
                pe.wait_ge(s_hot, it + 1)
                for m in range(4):
                    mm = pe.matmul(bank[7][:, 0:P], oh_lo[:, m, :], oh_hi[:, m, :], start=(first and m == 0), stop=(last and m == 3))
                mm.then_inc(s_list, 1)

            def phase_a(it, first, second=False):
                if not first:
                    pe.wait_ge(s_gev, it)
                for j in range(2):
                    pe.wait_ge(s_xt[j], (it + 1) * 16)
                    for k in range(HC):
                        mm = pe.matmul(bank[4][:, j * E:(j + 1) * E], xt_sb[j][:, k * P:(k + 1) * P], gatec[:, k, :],
                                       start=(k == 0), stop=(k == HC - 1))
                mm.then_inc(s_g, 1)
                if not first:
                    ranks(it - 1)
                pe.wait_ge(s_gev, it + 1)
                for j in range(2):
                    pe.wait_ge(s_bd[j], (it + 1) * 2)
                    mm = pe.matmul(bank[5][:, j * E:(j + 1) * E], bd[j][:, :], g_sb[:, j * E:(j + 1) * E], start=True, stop=True)
                mm.then_inc(s_l, 1)
                for j in range(2):
                    if not first:
                        pe.wait_ge(s_cev[j], it * 2)
                    pe.wait_ge(s_x[j], (it + 1) * 16)
                    for h in range(2):
                        mm = pe.matmul(bank[2 * j + h][:, :], bd[j][:, :], x_sb[j][:, h * HALF:(h + 1) * HALF], start=True, stop=True)
                    mm.then_inc(s_c[j], 1)
                if not first:
                    lists(it - 1, second, False)

            phase_a(0, True)
            phase_a(1, False, True)
            with pe.Fori(2, NT // 2) as it:
                phase_a(it, False)
            ranks(NT // 2 - 1)
            lists(NT // 2 - 1, False, True)
            pe.wait_ge(s_gev, NT // 2)
            pe.matmul(bank[4][:, 0:E], ones, acc[:, :], start=True, stop=True).then_inc(s_cnt, 1)
            pe.wait_ge(s_cxx, 1)
            for q in range(4):
                mm = pe.matmul(bank[4 + q][:, :], c("ones", B),
                               ctxx[:, q * 8:(q + 1) * 8, :].rearrange("p n o -> p (n o)"), start=True, stop=True)
            mm.then_inc(s_cxb, 1)

            for j in range(2):
                pe.wait_ge(s_cev[j], NT)

            def transposes(g):
                pe.wait_ge(s_xg, (g + 1) * 16)
                for half, (bk, s) in enumerate(((2, s_ta), (3, s_tb))):
                    for k in range(4):
                        at = half * 4 + k
                        mm = pe.transpose(bank[bk][:, k * P:(k + 1) * P], xg[:, at * P:(at + 1) * P], ident)
                    mm.then_inc(s, 1)

            transposes(0)
            pe.wait_ge(s_cum, 1)

            def product(k, to, wh, wl, cols):
                for n, (a, b) in enumerate(((l_lo, wh), (l_hi, wh), (l_hi, wl))):
                    mm = pe.matmul(to[:, :], a[:, k, :], b[:, k, cols * HALF:(cols + 1) * HALF],
                                   start=(k == 0 and n == 0), stop=(k == HC - 1 and n == 2))
                return mm

            def slot(g, t, e, odd, first):
                if first:
                    pe.wait_ge(s_lo, (e + 1) * HC)
                pe.wait_ge(s_e0, g + CREDIT)
                pe.wait_ge(s_la, g + 1)
                for k in range(HC):
                    if k == 4:
                        pe.wait_ge(s_lb, g + 1)
                    mm = product(k, bank[0], w_hi[odd], w_lo[odd], 0)
                mm.then_inc(s_h0, 1)
                transposes(g + 1)
                pe.wait_ge(s_e1, g + CREDIT)
                for k in range(HC):
                    mm = product(k, bank[1], w_hi[odd], w_lo[odd], 1)
                    if k == 3:
                        mm.then_inc(s_fa, 1)
                mm.then_inc(s_h1, 1)

            slots(pe, slot)

            total = pe.value_load(cum[0:1, E:E + 1], min_val=E, max_val=SLOTS)
            pe.wait_ge(s_late, 64)
            pe.wait_ge(s_cx, 4)
            pe.wait_ge(s_e0, total + CREDIT)
            pe.wait_ge(s_e1, total + CREDIT)
            wait_apart(pe, s_lb, total + 1)

            def conv(t, rel, free):
                pe.wait_ge(s_rel, rel)
                if free is not None:
                    pe.wait_ge(s_c1, free)
                for b in range(2):
                    for u in range(CQ):
                        for m in range(MC):
                            at = (u * MC + m) * P
                            for k in range(WINS):
                                mm = pe.matmul(bank[4 + b][:, at:at + P], x1p[:, b, u, m * P + k:(m + 1) * P + k],
                                               conv_sb[:, k, u, :], start=(k == 0), stop=(k == WINS - 1))
                    mm.then_inc(s_cv, 1)

            def down(t):
                pe.wait_ge(s_c1, (t + 1) * 2)
                pe.wait_ge(s_g1e, t + CREDIT)
                for k in range(HC):
                    mm = pe.matmul(bank[2][:, 0:G1W], c1[:, k, :], down_sb[:, k, :], start=(k == 0), stop=(k == HC - 1))
                mm.then_inc(s_g1, 1)

            def main(t, last=False):
                for h, (s, done) in enumerate(((s_m0, s_me0), (s_m1, s_me1))):
                    if last and h == 1:
                        pe.wait_ge(s_a2, NT + CREDIT)
                        pe.matmul(bank[2][:, 0:2 * E], ones, acc2[:, :], start=True, stop=True).then_inc(s_t2, 1)
                    pe.wait_ge(done, t + CREDIT)
                    for k in range(HC):
                        if h == 0 and k % 4 == 0:
                            pe.wait_ge(s_cl, t * 2 + k // 4 + 1)
                        mm = product(k, bank[h], w_hi[0], w_lo[0], h)
                    mm.then_inc(s, 1)

            conv(0, 16, None)
            with pe.Fori(0, NT - 1) as t:
                down(t)
                conv(t + 1, (t + 2) * 16, (t + 1) * 2)
                main(t)
            down(NT - 1)
            main(NT - 1, True)

            for q in range(TQ):
                pe.wait_ge(s_tw, q + 1)
                for t in range(q * TG, (q + 1) * TG):
                    mm = pe.transpose(bank[4 + q][:, (t % TG) * P:(t % TG + 1) * P], down_all[:, t, :], ident)
                mm.then_inc(s_twt, 1)
            pe.wait_ge(s_ul, 2)
            for t in range(NT):
                q, at = t // TG, (t % TG) * P
                if t % TG == 0:
                    pe.wait_ge(s_tl, q + 1)
                if t == 1:
                    pe.wait_ge(s_me1, NT + CREDIT)
                if t >= 2:
                    pe.wait_ge(s_fin, (t - 1) * 2)
                for h in range(2):
                    for n, (a, b) in enumerate(((twt_lo, up_hi), (twt_hi, up_hi), (twt_hi, up_lo))):
                        mm = pe.matmul(bank[2 * (1 - t % 2) + h][:, :], a[:, q, at:at + P], b[:, h, :], start=(n == 0), stop=(n == 2))
                    mm.then_inc(s_up, 1)


INPUTS = ["x", "x_t", "consts_a", "consts_b", "expert_w", "conv_w", "down_w", "lora_b"]


def lay_out(i):
    f = np.float32
    a = np.zeros((P, CA_W), f)
    b = np.zeros((P, CB_W), f)

    def put(to, where, name, v):
        lo, hi = where[name]
        to[:, lo:hi] = np.reshape(v, (-1, hi - lo)) if np.ndim(v) else v

    put(a, CA, "emb", i["cond_128"].T)
    put(a, CA, "w0", i["L0_cond_W0"])
    put(a, CA, "w1", i["L0_cond_W1"])
    put(a, CA, "w2", i["L0_cond_W2"])
    put(a, CA, "b0", i["L0_cond_b0"][:, None])
    put(a, CA, "b1", i["L0_cond_b1"][:, None])
    put(a, CA, "b2", np.broadcast_to(i["L0_cond_b2"], (P, K8)))
    put(a, CA, "gate", i["L0_ffn_gate_w"].reshape(HC, P, E).transpose(1, 0, 2).reshape(P, -1))
    kern = i["L0_cond_weight"][..., 0].transpose(2, 0, 1).reshape(CH, -1)
    put(a, CA, "kern", np.concatenate([kern, kern]))
    put(a, CA, "kbias", np.concatenate([i["L0_cond_bias_k"].T] * 2))
    put(a, CA, "ident", np.eye(P, dtype=f))
    put(a, CA, "tri", np.triu(np.ones((P, P), f), 1))
    put(a, CA, "ones", np.ones((P, P), f))
    put(a, CA, "iota", np.broadcast_to(np.arange(P, dtype=f), (P, P)))
    put(a, CA, "thr", np.broadcast_to(np.arange(1, NT, dtype=f) * P, (P, NT - 1)))
    put(a, CA, "cw", i["L1_cond_c_weight"].T)
    put(a, CA, "fside", np.broadcast_to(i["fside_S_0"], (P, CH)))
    put(a, CA, "tok", np.arange(NT, dtype=f)[None, :] * P + np.arange(P, dtype=f)[:, None])
    put(b, CB, "gb1", np.broadcast_to(i["L1_ffn_gb1"], (P, HG)))
    put(b, CB, "gamma", np.broadcast_to(i["L1_ffn_ln_gamma"], (P, HG)))
    put(b, CB, "beta", np.broadcast_to(i["L1_ffn_ln_beta"], (P, HG)))
    put(b, CB, "gb2", np.broadcast_to(i["L1_ffn_gb2"], (P, E)))
    put(b, CB, "gw2", np.broadcast_to(i["L1_ffn_gw2"].reshape(-1), (P, E * HG)))

    w = i["L1_cond_weight"]
    per = w.shape[1]
    conv = np.zeros((PH, CP, WINS, CQ, PH, CP), f)
    for qi in range(PH):
        for qo in range(PH):
            for k in range(WINS):
                tap = PH * k + qi - qo
                if 0 <= tap < TAPS:
                    for g in range(CH // per):
                        u, at = divmod(g * per, CP)
                        s = slice(at, at + per)
                        conv[qi, s, k, u, qo, s] = w[g * per:(g + 1) * per, :, tap].T

    def by_phase(m):
        return m.reshape(MC, P, PH, -1).transpose(1, 0, 2, 3).reshape(P, HC, -1)

    down = np.concatenate([by_phase(i["L1_ffn_lora_A"].transpose(1, 0, 2).reshape(H, E * R)),
                           by_phase(i["L1_ffn_gw1"].T)], axis=2)
    x = i["x"].reshape(N, H)
    return {
        "x": x,
        "x_t": x.reshape(NT, P, HC, P).transpose(0, 3, 2, 1).reshape(NT * P, H),
        "consts_a": a,
        "consts_b": b,
        "expert_w": np.concatenate([i["L0_ffn_expert_w"].reshape(E, HC, P, H),
                                    by_phase(i["L1_ffn_weight"].T).transpose(1, 0, 2)[None]]),
        "conv_w": conv.reshape(P, WINS, CQ, P),
        "down_w": down,
        "lora_b": i["L1_ffn_lora_B"].reshape(E * R, H),
    }


def kernel(**inputs):
    import concourse.bacc as bacc
    from concourse.bass_utils import run_bass_kernel_spmd

    nc = bacc.Bacc("TRN2", target_bir_lowering=False, num_devices=1)
    laid = lay_out({k: np.asarray(v) for k, v in inputs.items()})
    arrays, args = {}, []
    for name in INPUTS:
        a = np.ascontiguousarray(laid[name])
        arrays[f"in_{name}"] = a
        args.append(nc.dram_tensor(f"in_{name}", a.shape, mybir.dt.from_np(a.dtype), kind="ExternalInput").ap())
    out = nc.dram_tensor("out_0", (N, H), F32, kind="ExternalOutput").ap()
    build(nc, *args, out)
    r = run_bass_kernel_spmd(nc, [arrays], core_ids=[0])
    return r.results[0]["out_0"].reshape(B, CH, H)
```

```python
from contextlib import ExitStack

import numpy as np

import concourse.bass as bass
from concourse import mybir

ALU = mybir.AluOpType
ACT = mybir.ActivationFunctionType
AX = mybir.AxisListType
F32 = mybir.dt.float32
F32R = mybir.dt.float32r
I32 = mybir.dt.int32
U32 = mybir.dt.uint32

P = 128
B, CH, H = 32, 64, 1024
N = B * CH
NT = N // P
E = 8
K8 = 8
SLOTS = 2 * NT + E - 1
HC = H // P
HALF = H // 2
R = 16
HG = 4 * E
TAPS, PAD = 9, 4
PH = 8
CP = P // PH
CQ = CH // CP
WINS = (TAPS - 1 + PH - 1) // PH + 1
MW = (H + 2 * PAD) // PH
MC = H // PH // P
CAPACITY = int(3.0 * N / E)
ALPHA = 1.0 / R
RING = 4
TQ = NT * P // HALF
TG = NT // TQ
LN_EPS = 1e-5
CREDIT, DMA_CREDIT = 1, 16
G1W = E * R + HG


def columns(widths):
    at, out = 0, {}
    for name, w in widths:
        out[name] = (at, at + w)
        at += w
    return out, at


CA, CA_W = columns([("emb", B), ("w0", P), ("w1", P), ("w2", K8), ("b0", 1), ("b1", 1), ("b2", K8),
                    ("gate", HC * E), ("kern", K8 * CH), ("kbias", K8), ("ident", P), ("tri", P),
                    ("ones", P), ("iota", P), ("thr", NT - 1), ("cw", CH), ("fside", CH), ("tok", NT)])
CB, CB_W = columns([("gb1", HG), ("gamma", HG), ("beta", HG), ("gb2", E), ("gw2", E * HG)])


class Chain:

    def __init__(self, eng, sem, base=0):
        self.eng, self.sem, self.base, self.n = eng, sem, base, 0

    def add(self, ins):
        ins.then_inc(self.sem, 1)
        self.n += 1
        return self.n

    def wait(self, n=None):
        self.eng.wait_ge(self.sem, self.base + (self.n if n is None else n))

    def link(self, ins):
        self.add(ins)
        self.wait()


def build(nc, x, x_t, x_ph, consts_a, consts_b, expert_w, conv_w, down_w, lora_b, out):
    ctx = ExitStack()
    with ctx:
        def sb(name, shape, dt=F32):
            return ctx.enter_context(nc.sbuf_tensor(name, shape, dt))

        def sem(name):
            return ctx.enter_context(nc.semaphore(name))

        def dram(name, shape, dt=F32):
            return nc.dram_tensor(name, shape, dt, kind="Internal").ap()

        c0_d = dram("c0_scratch", [N, H])
        x1_d = dram("x1_scratch", [N, H])
        y_d = dram("y_scratch", [(SLOTS + 1) * P, H])

        CTX_BANKS = (2, 3, 6, 7)
        bank = [ctx.enter_context(nc.psum_tensor(f"bank{i}", [P, 512], F32)) for i in range(8)]

        ca = sb("ca", [P, CA_W])
        cb = sb("cb", [P, CB_W])
        conv_sb = sb("conv_sb", [P, WINS, CQ, P])
        down_sb = sb("down_sb", [P, HC, G1W])
        lora_sb = sb("lora_sb", [P, H])

        def c(name, rows=P):
            a, b = CA[name]
            return ca[0:rows, a:b]

        def d(name):
            a, b = CB[name]
            return cb[:, a:b]

        with nc.sbuf_tensor("weights_1", [P, 2, HC, H], F32R) as weights_1:
            pass
        res = sb("res", [P, NT, H])
        weights = [sb("weights_0", [P, 2, HC, H], F32R), weights_1]
        w_hi = [w[:, 0] for w in weights]
        w_lo = [w[:, 1] for w in weights]
        sel = res[:, NT - 4, 0:2 * NT * E].rearrange("p (t e) -> p t e", e=E)
        cmp = res[:, NT - 4, 2 * NT * E:2 * NT * E + E * (NT - 1)].rearrange("p (e t) -> p e t", e=E)
        prod = res[:, NT - 5, :].rearrange("p (k o) -> p k o", o=CH).rearrange("p (j k) o -> p j k o", j=2)
        aggb_t = res[:, NT - 3, 0:NT * K8].rearrange("p (t k) -> p t k", k=K8)
        l_hi = sb("l_hi", [P, HC, P], F32R)
        l_lo = sb("l_lo", [P, HC, P], F32R)
        work = sb("work", [P, 8 * H])

        def row(i, n=1):
            return work[:, i * H:(i + n) * H]

        x_sb = [[row(0), row(1)], [res[:, 0, :], res[:, 1, :]]]
        xt_sb = [[row(2), row(3)], [res[:, 2, :], res[:, 3, :]]]
        xt_pair = [row(2, 2).rearrange("p (j k m) -> p k j m", j=2, k=HC),
                   res[:, 2:4, :].rearrange("p j (k m) -> p k j m", k=HC)]
        c0_sb = [row(4), row(5)]
        raw0 = row(6)
        oh_lo = row(7)[:, 0:4 * P].rearrange("p (m n) -> p m n", m=4)
        oh_hi = row(7)[:, 4 * P:8 * P].rearrange("p (m n) -> p m n", m=4)
        raw = [row(i) for i in range(4)]
        yo = row(6)
        xg = row(7)
        yg = [row(0, 2).rearrange("p (k n) -> p k n", k=2),
              row(2, 2).rearrange("p (k n) -> p k n", k=2)]
        ring = [row(j) for j in range(RING)]
        c1 = row(4).rearrange("p (c m) -> p c m", c=HC)
        down_all = row(6, 2).rearrange("p (t n) -> p t n", t=NT)
        x1p = sb("x1p", [P, 2, CQ, MW])
        ctxb = sb("ctxb", [P, B, CH])

        warm = sb("warm", [P, 2])
        h0 = sb("h0", [P, B])
        h1 = sb("h1", [P, B])
        at_l = sb("at_l", [B, K8])
        at_m = sb("at_m", [B, 1])
        at_n = sb("at_n", [B, 1])
        at_e = sb("at_e", [B, K8])
        at_s = sb("at_s", [B, 1])
        at_r = sb("at_r", [B, 1])
        att = sb("att", [B, K8])
        scratch = sb("scratch", [P, E * HG])
        attx = scratch[0:B, :].rearrange("p (n k) -> p n k", k=K8)
        attp = sb("attp", [P, NT * K8])
        gsum = sb("gsum", [P, E])
        aggb = sb("aggb", [P, NT])
        agg = sb("agg", [P, 2, CH])
        bd = [sb(f"bd{j}", [P, P]) for j in range(2)]
        gt_sb = res[0:E, NT - 6, 0:2 * P]
        g_sb = sb("g_sb", [P, 2 * E])
        lg = sb("lg", [P, 2, E])
        mx = sb("mx", [P, 2, 8])
        ix = sb("ix", [P, 2, 8], U32)
        mx_all = sb("mx_all", [P, NT, 2])
        ixf = sb("ixf", [P, 4])
        oh = sb("oh", [P, 2, 2, E])
        msk = sb("msk", [P, 2, E])
        pre = sb("pre", [P, 2, E])
        acc = sb("acc", [P, E])
        rk = sb("rk", [P, 2, 2, E])
        rk4 = sb("rk4", [P, 4])
        pos_s = sb("pos_s", [P, 4], I32)
        lo_i = sb("lo_i", [P, 4], I32)
        hi_i = sb("hi_i", [P, 4], I32)
        lo_f = sb("lo_f", [P, 4])
        hi_f = sb("hi_f", [P, 4])
        idx_all = sb("idx_all", [P, P], I32)
        rank_all = sb("rank_all", [P, 2 * NT])
        ix_all = sb("ix_all", [P, 2 * NT])
        base_f = sb("base_f", [P, 2 * NT])
        pos_all = sb("pos_all", [P, NT * 2], I32)
        tl = sb("tl", [P, E])
        cumf = sb("cumf", [P, E + 1])
        cum = sb("cum", [P, E + 1], I32)
        cnt = sb("cnt", [P, E + 1], I32)
        wd = sb("wd", [P, NT])
        we = sb("we", [P, NT])
        ws = sb("ws", [P, NT])
        w_all = sb("w_all", [P, NT, 2])
        idx = sb("idx", [P, 1], I32)
        ctx0 = sb("ctx0", [B, CH])
        ctxx = row(4, 2)[0:B, :].rearrange("p (n o) -> p n o", o=CH)
        pos_c = [sb(f"pos_c{j}", [P, 2], I32) for j in range(2)]
        hb = sb("hb", [P, HG])
        st = sb("st", [P, 6])
        mv = sb("mv", [P, 2])
        ve = sb("ve", [P, 1])
        sd = sb("sd", [P, 1])
        rs = sb("rs", [P, 1])
        hn = sb("hn", [P, HG])
        hp = scratch[:, :].rearrange("p (e h) -> p e h", h=HG)
        gl = sb("gl", [P, E])
        gt = sb("gt", [P, E])
        mx2 = sb("mx2", [P, 8])
        ix2 = sb("ix2", [P, 8], U32)
        ixf2 = sb("ixf2", [P, 2])
        mx2_all = row(5)[:, 2 * NT:4 * NT].rearrange("p (t k) -> p t k", k=2)
        oh_all = row(5)[:, 4 * P:4 * P + 2 * NT * E].rearrange("p (t k e) -> p t k e", t=NT, k=2)
        acc2 = sb("acc2", [P, 2 * E])
        allow = sb("allow", [P, 2 * E])
        g2 = row(5)[:, 0:2 * NT].rearrange("p (t k) -> p t k", k=2)
        w2_all = row(5)[:, 6 * P:6 * P + NT * E].rearrange("p (t e) -> p t e", e=E)
        up_hi, up_lo = w_hi[0][:, 0:2, 0:HALF], w_lo[0][:, 0:2, 0:HALF]
        twt_hi, twt_lo = w_hi[0][:, 2:2 + TQ, 0:HALF], w_lo[0][:, 2:2 + TQ, 0:HALF]

        s_apart = sem("s_apart")
        s_mlp = sem("s_mlp")
        s_const = sem("s_const")
        s_x = [[sem(f"s_x_{p}_{j}") for j in range(2)] for p in range(2)]
        s_xt = [[sem(f"s_xt_{p}_{j}") for j in range(2)] for p in range(2)]
        s_raw0 = sem("s_raw0")
        s_raw = [sem(f"s_raw_{j}") for j in range(4)]
        s_hi = sem("s_hi")
        s_lo = sem("s_lo")
        s_late = sem("s_late")
        s_pe0 = sem("s_pe0")
        s_act0 = sem("s_act0")
        s_dve0 = sem("s_dve0")
        s_init = sem("s_init")
        s_attx = sem("s_attx")
        s_sm = sem("s_sm")
        s_agg = sem("s_agg")
        s_bd = [sem(f"s_bd_{j}") for j in range(2)]
        s_g = sem("s_g")
        s_gt = sem("s_gt")
        s_gg = sem("s_gg")
        s_gev = sem("s_gev")
        s_l = sem("s_l")
        s_m = sem("s_m")
        s_r = sem("s_r")
        s_c = [sem(f"s_c_{j}") for j in range(2)]
        s_cev = [sem(f"s_cev_{j}") for j in range(2)]
        s_cst = [sem(f"s_cst_{j}") for j in range(2)]
        s_hot = sem("s_hot")
        s_list = sem("s_list")
        s_chA = sem("s_chA")
        s_cnt = sem("s_cnt")
        s_ids = sem("s_ids")
        s_cum = sem("s_cum")
        s_chB = sem("s_chB")
        s_wd = sem("s_wd")
        s_we = sem("s_we")
        s_cxx = sem("s_cxx")
        s_cxb = sem("s_cxb")
        s_cx = sem("s_cx")
        s_rest = sem("s_rest")
        s_idx = sem("s_idx")
        s_xg = sem("s_xg")
        s_ta = sem("s_ta")
        s_tb = sem("s_tb")
        s_ha = sem("s_ha")
        s_hb = sem("s_hb")
        s_la = sem("s_la")
        s_lb = sem("s_lb")
        s_fa = sem("s_fa")
        s_h0 = sem("s_h0")
        s_h1 = sem("s_h1")
        s_e0 = sem("s_e0")
        s_e1 = sem("s_e1")
        s_y0 = sem("s_y0")
        s_y1 = sem("s_y1")
        s_pad = sem("s_pad")
        s_pall = sem("s_pall")
        s_pc = sem("s_pc")
        s_yg = [[sem(f"s_yg_{j}_{k}") for k in range(2)] for j in range(2)]
        s_xr = [sem(f"s_xr_{j}") for j in range(2)]
        s_chC = sem("s_chC")
        s_x1 = sem("s_x1")
        s_x1d = sem("s_x1d")
        s_rel = sem("s_rel")
        s_cv = sem("s_cv")
        s_c1 = sem("s_c1")
        s_ch = sem("s_ch")
        s_cl = sem("s_cl")
        s_g1 = sem("s_g1")
        s_g1e = sem("s_g1e")
        s_ve = sem("s_ve")
        s_sd = sem("s_sd")
        s_m0 = sem("s_m0")
        s_m1 = sem("s_m1")
        s_me0 = sem("s_me0")
        s_me1 = sem("s_me1")
        s_a2 = sem("s_a2")
        s_t2 = sem("s_t2")
        s_chD = sem("s_chD")
        s_d2 = sem("s_d2")
        s_ex2 = sem("s_ex2")
        s_tw = sem("s_tw")
        s_twt = sem("s_twt")
        s_th = sem("s_th")
        s_tl = sem("s_tl")
        s_uh = sem("s_uh")
        s_ul = sem("s_ul")
        s_up = sem("s_up")
        s_fin = sem("s_fin")
        s_out = [sem(f"s_out_{j}") for j in range(RING)]

        tile_rows = lambda t: bass.ds(t * P, P)

        block = ctx.enter_context(nc.Block())

        def slots(eng, body):
            with eng.Fori(0, E // 2) as pair:
                for odd in range(2):
                    e = pair * 2 + odd
                    first = eng.value_load(cum[0:1, bass.ds(e, 1)], min_val=0, max_val=SLOTS)
                    count = eng.value_load(cnt[0:1, bass.ds(e, 1)], min_val=1, max_val=NT)
                    body(first, 0, e, odd, True)
                    with eng.Fori(1, count) as t:
                        body(first + t, t, e, odd, False)

        def wait_apart(eng, sem_, value):
            eng.wait_ge(sem_, value)
            eng.sem_inc(s_apart, 1)

        @block.sync
        def _(sp):
            for credited in (s_y0, s_y1, s_cst[0], s_cst[1], *s_out):
                sp.sem_inc(credited, DMA_CREDIT)
            for credited in (s_e0, s_e1, s_tb, s_g1e, s_me0, s_me1, s_a2):
                sp.sem_inc(credited, CREDIT)
            mlp = CA["b2"][1]
            sp.dma_start(ca[:, 0:mlp], consts_a[:, 0:mlp]).then_inc(s_mlp, 16)
            sp.dma_start(ca[:, mlp:CA_W], consts_a[:, mlp:CA_W]).then_inc(s_const, 16)

            def load_x(rows, p, j):
                sp.dma_start(x_sb[p][j], x[rows, :]).then_inc(s_x[p][j], 16)

            def load_xt(rows, p, j):
                sp.dma_start(xt_sb[p][j], x_t[rows, :]).then_inc(s_xt[p][j], 16)

            def load_raw0(k):
                sp.dma_start(raw0, expert_w[0, k, :, :].rearrange("o p n -> p (o n)")).then_inc(s_raw0, 16)

            for p in range(2):
                for j in range(2):
                    load_xt(tile_rows(2 * p + j), p, j)
                for j in range(2):
                    load_x(tile_rows(2 * p + j), p, j)
                if p == 0:
                    load_raw0(bass.ds(0, 1))

            def phase_a(it, p, row0, ahead, nxt):
                if ahead is not None:
                    sp.wait_ge(s_g, it + 1)
                    for j in range(2):
                        load_xt(bass.ds(ahead[j], P), p, j)
                for j in range(2):
                    if ahead is not None:
                        sp.wait_ge(s_c[j], it + 1)
                        load_x(bass.ds(ahead[j], P), p, j)
                    sp.wait_ge(s_cev[j], 2 * (it + 1))
                    sp.dma_start(c0_d[bass.ds(row0[j], P), :], c0_sb[j]).then_inc(s_cst[j], 16)
                if nxt is not None:
                    sp.wait_ge(s_lo, it + 1)
                    load_raw0(nxt)

            with sp.Fori(0, NT // 4 - 1) as i:
                row0 = [[sp.snap((i * 4 + 2 * p + j) * P) for j in range(2)] for p in range(2)]
                ahead = [[sp.snap((i * 4 + 4 + 2 * p + j) * P) for j in range(2)] for p in range(2)]
                nxt = [bass.ds(sp.snap(i * 2 + p + 1), 1) for p in range(2)]
                for p in range(2):
                    phase_a(i * 2 + p, p, row0[p], ahead[p], nxt[p])
            for p in range(2):
                it = NT // 2 - 2 + p
                phase_a(it, p, [(it * 2 + j) * P for j in range(2)], None, bass.ds(it + 1, 1) if p == 0 else None)

            def load_raw(e, half):
                for k in range(HC // 2):
                    sp.dma_start(raw[k], expert_w[e, half * (HC // 2) + k, :, :].rearrange("o p n -> p (o n)")).then_inc(s_raw[k], 16)

            for j in range(2):
                sp.wait_ge(s_c[j], NT // 2)
            sp.wait_ge(s_xg, 16)
            load_raw(bass.ds(1, 1), 0)
            for j in range(2):
                sp.wait_ge(s_cst[j], 16 * (NT // 2) + DMA_CREDIT)
            sp.wait_ge(s_cum, 1)

            def store0(g, rows):
                sp.wait_ge(s_e0, g + 1 + CREDIT)
                sp.dma_start(y_d[rows, 0:HALF], yo[:, 0:HALF]).then_inc(s_y0, 16)

            def store1(g, rows):
                sp.wait_ge(s_e1, g + 1 + CREDIT)
                sp.dma_start(y_d[rows, HALF:H], yo[:, HALF:H]).then_inc(s_y1, 16)

            def expert(e, last):
                first = sp.value_load(cum[0:1, bass.ds(e, 1)], min_val=0, max_val=SLOTS - 1)
                end = sp.value_load(cum[0:1, bass.ds(e + 1, 1)], min_val=1, max_val=SLOTS)
                second = sp.snap(first + 1)
                rows = bass.ds(sp.snap(first * P), P)
                nxt = bass.ds(sp.snap(e * 1 + 1), 1)
                nxt2 = None if last else bass.ds(sp.snap(e * 1 + 2), 1)
                sp.wait_ge(s_lo, (e + 1) * HC + HC // 2)
                load_raw(nxt, 1)
                store0(first, rows)
                store1(first, rows)
                if not last:
                    sp.wait_ge(s_lo, (e + 1) * HC + HC)
                    load_raw(nxt2, 0)
                with sp.Fori(second, end) as g:
                    rows = bass.ds(sp.snap(g * P), P)
                    store0(g, rows)
                    store1(g, rows)

            with sp.Fori(0, 1) as e:
                expert(e, False)
            with sp.Fori(sp.value_load(cum[0:1, E:E + 1], min_val=E, max_val=SLOTS), SLOTS + 1) as g:
                sp.dma_start(y_d[bass.ds(sp.snap(g * P), P), :], c0_sb[0]).then_inc(s_rest, 16)
            sp.dma_start(cb[:, :], consts_b).then_inc(s_late, 16)
            sp.dma_start(conv_sb[:, :, :, :], conv_w).then_inc(s_late, 16)
            sp.dma_start(down_sb[:, :, :], down_w).then_inc(s_late, 16)
            sp.dma_start(lora_sb[:, :], lora_b).then_inc(s_late, 16)
            with sp.Fori(1, E - 1) as e:
                expert(e, False)
            with sp.Fori(E - 1, E) as e:
                expert(e, True)

            total = sp.value_load(cum[0:1, E:E + 1], min_val=E, max_val=SLOTS)
            unused = sp.value_load(cnt[0:1, E:E + 1], min_val=1, max_val=SLOTS + 1)
            wait_apart(sp, s_rest, unused * 16)
            sp.wait_ge(s_h1, total)

            def load_res(t, at, j):
                sp.dma_start(res[:, bass.ds(at, 1), :].rearrange("p o n -> p (o n)"), x_ph[bass.ds(t, P), :]).then_inc(s_xr[j], 16)

            def rearrange(t0, at, x1, stored, free):
                rows = bass.ds(t0, P)
                sp.wait_ge(s_x1, x1)
                sp.dma_start(x1_d[rows, :], res[:, bass.ds(at, 1), :].rearrange("p o n -> p (o n)")).then_inc(s_x1d, 16)
                wait_apart(sp, s_x1d, stored)
                if free is not None:
                    sp.wait_ge(s_cv, free)
                by_phase = x1_d[rows, :].rearrange("(u c) (q w) -> q c u w", c=CP, q=PH)
                for q in range(PH):
                    a = q // (PH // 2)
                    sp.dma_start(x1p[q * CP:(q + 1) * CP, :, :, a:a + MW - 1].rearrange("c b u w -> c (b u) w"),
                                 by_phase[q]).then_inc(s_rel, 16)

            load_res(0, 0, 0)
            for k in range(2):
                sp.wait_ge(s_yg[0][k], 16)
            load_res(P, 1, 1)
            rearrange(0, 0, 1, 16, None)
            load_res(2 * P, 2, 0)
            rearrange(P, 1, 2, 32, 2)
            load_res(3 * P, 3, 1)
            with sp.Fori(1, NT // 2 - 1) as i:
                t0 = [sp.snap((i * 2 + j) * P) for j in range(2)]
                at = [sp.snap(i * 2 + j) for j in range(2)]
                counts = [[sp.snap(i * 2 + j + 1), sp.snap((i * 2 + j + 1) * 16), sp.snap((i * 2 + j) * 2)] for j in range(2)]
                ahead = [(sp.snap((i * 2 + j + 2) * P), sp.snap(i * 2 + j + 2)) for j in range(2)]
                for j in range(2):
                    sp.wait_ge(s_xr[j], (i + 1) * 16)
                    load_res(ahead[j][0], ahead[j][1], j)
                    rearrange(t0[j], at[j], *counts[j])
            for t in range(NT - 2, NT):
                rearrange(t * P, t, t + 1, (t + 1) * 16, t * 2)
            with sp.Fori(0, NT // RING) as i:
                rows = [bass.ds(sp.snap((i * RING + j) * P), P) for j in range(RING)]
                for j in range(RING):
                    sp.wait_ge(s_fin, (i * RING + j) * 2 + 2)
                    sp.dma_start(out[rows[j], :], ring[j]).then_inc(s_out[j], 16)
            for j in range(RING):
                sp.wait_ge(s_out[j], 16 * (NT // RING) + DMA_CREDIT)

        @block.gpsimd
        def _(pool):
            for j in range(2):
                pool.memset(bd[j][:, :], 0.0).then_inc(s_init, 1)
            pool.memset(acc[:, :], 0.0).then_inc(s_init, 1)
            pool.memset(acc2[:, :], 0.0).then_inc(s_init, 1)
            pool.memset(cumf[:, 0:1], 0.0).then_inc(s_init, 1)
            pool.wait_ge(s_init, 5)
            pool.memset(x1p[0:P // 2, :, :, MW - 1:MW], 0.0).then_inc(s_pad, 1)
            pool.wait_ge(s_pad, 1)
            pool.memset(x1p[P // 2:P, :, :, 0:1], 0.0).then_inc(s_pad, 1)
            pool.wait_ge(s_pad, 2)

            def rest0(it):
                wait_apart(pool, s_hi, it + 1)
                at = bass.ds(it, 1)
                pool.tensor_tensor(w_lo[0][:, at, :].rearrange("p o n -> p (o n)"), raw0,
                                   w_hi[0][:, at, :].rearrange("p o n -> p (o n)").bitcast(F32), ALU.subtract).then_inc(s_lo, 1)

            with pool.Fori(0, NT // 2) as it:
                rest0(it)
            pool.wait_ge(s_ids, 1)
            for j in range(2):
                pool.wait_ge(s_cst[j], 16 * (NT // 2) + DMA_CREDIT)

            def gather():
                pool.indirect_dma_start(xg, None, c0_d, bass.IndirectOffsetOnAxis(ap=idx[:, 0:1], axis=0)).then_inc(s_xg, 16)

            pool.tensor_copy(idx[:, :], idx_all[:, 0:1]).then_inc(s_idx, 1)
            pool.wait_ge(s_idx, 1)
            gather()
            pool.wait_ge(s_xg, 16)
            pool.wait_ge(s_cum, 1)

            def fetch_slots(e, start):
                first = pool.value_load(cum[0:1, bass.ds(e, 1)], min_val=0, max_val=SLOTS)
                count = pool.value_load(cnt[0:1, bass.ds(e, 1)], min_val=1, max_val=NT)
                with pool.Fori(start, count) as t:
                    g = first + t
                    pool.tensor_copy(idx[:, :], idx_all[:, bass.ds(pool.snap(e * NT + t), 1)]).then_inc(s_idx, 1)
                    wait_apart(pool, s_idx, g + 1)
                    wait_apart(pool, s_tb, g + CREDIT)
                    gather()
                    wait_apart(pool, s_xg, (g + 1) * 16)

            with pool.Fori(0, 1) as e:
                fetch_slots(e, 1)
            with pool.Fori(1, E) as e:
                fetch_slots(e, 0)
            total = pool.value_load(cum[0:1, E:E + 1], min_val=E, max_val=SLOTS)
            wait_apart(pool, s_tb, total + CREDIT)
            gather()
            pool.wait_ge(s_pall, 1)
            pool.wait_ge(s_lo, (E + 1) * HC)
            wait_apart(pool, s_y0, total * 16 + DMA_CREDIT)
            wait_apart(pool, s_y1, total * 16 + DMA_CREDIT)

            def fetch(t, j, it):
                pool.tensor_copy(pos_c[j][:, :], pos_all[:, bass.ds(t * 2, 2)]).then_inc(s_pc, 1)
                wait_apart(pool, s_pc, t + 1)
                for k in range(2):
                    pool.indirect_dma_start(yg[j][:, k, :], None, y_d,
                                            bass.IndirectOffsetOnAxis(ap=pos_c[j][:, k:k + 1], axis=0)).then_inc(s_yg[j][k], 16)

            fetch(0, 0, 0)
            fetch(1, 1, 0)
            pool.wait_ge(s_rel, PH * 16)
            with pool.Fori(1, NT // 2) as i:
                for j in range(2):
                    wait_apart(pool, s_x1, i * 2 + j - 1)
                    fetch(i * 2 + j, j, i)

        @block.scalar
        def _(act):
            act.wait_ge(s_init, 5)
            act.activation(warm[:, 0:1], acc[:, 0:1], ACT.Gelu)
            act.wait_ge(s_mlp, 16)
            act.wait_ge(s_pe0, 1)
            act.activation(h0[:, :], bank[0][:, 0:B], ACT.Gelu, bias=c("b0")).then_inc(s_act0, 1)
            act.wait_ge(s_pe0, 2)
            act.activation(h1[:, :], bank[1][:, 0:B], ACT.Gelu, bias=c("b1")).then_inc(s_act0, 1)
            act.activation(warm[:, 1:2], acc[:, 1:2], ACT.Exp)
            act.wait_ge(s_sm, 1)
            act.activation(at_e[:, :], at_l[:, :], ACT.Exp, bias=at_n[:, :], accum_out=at_s[:, :]).then_inc(s_act0, 1)

            def spread(j, it):
                act.wait_ge(s_agg, it + 1)
                act.activation(bd[j][0:CH, 0:CH], agg[0:CH, j, :], ACT.Copy).then_inc(s_bd[j], 1)
                act.activation(bd[j][CH:P, CH:P], agg[CH:P, j, :], ACT.Copy).then_inc(s_bd[j], 1)

            for j in range(2):
                spread(j, 0)

            def phase_a(it, last):
                act.wait_ge(s_raw0, (it + 1) * 16)
                act.activation(w_hi[0][:, bass.ds(it, 1), :].rearrange("p o n -> p (o n)"), raw0, ACT.Copy).then_inc(s_hi, 1)
                for j in range(2):
                    act.wait_ge(s_c[j], it + 1)
                    act.wait_ge(s_cst[j], it * 16 + DMA_CREDIT)
                    for h in range(2):
                        act.activation(c0_sb[j][:, h * HALF:(h + 1) * HALF], bank[2 * j + h][:, :], ACT.Identity,
                                       bias=aggb[:, bass.ds(it * 2 + j, 1)]).then_inc(s_cev[j], 1)
                if not last:
                    act.wait_ge(s_l, it + 1)
                    for j in range(2):
                        spread(j, it + 1)

            with act.Fori(0, NT // 2 - 1) as it:
                phase_a(it, False)
            phase_a(NT // 2 - 1, True)

            def round_a(g):
                act.wait_ge(s_ta, g + 1)
                act.wait_ge(s_fa, g)
                act.activation(l_hi[:, 0:4, :], bank[2][:, :].rearrange("p (c m) -> p c m", c=4), ACT.Copy).then_inc(s_ha, 1)

            def round_b(g):
                act.wait_ge(s_tb, g + 1 + CREDIT)
                act.wait_ge(s_h1, g)
                act.activation(l_hi[:, 4:8, :], bank[3][:, :].rearrange("p (c m) -> p c m", c=4), ACT.Copy).then_inc(s_hb, 1)

            def round_w(e, odd, half):
                for k in range(HC // 2):
                    act.wait_ge(s_raw[k], e * 32 + (half + 1) * 16)
                    act.activation(w_hi[1 - odd][:, half * (HC // 2) + k, :], raw[k], ACT.Copy).then_inc(s_hi, 1)

            round_a(0)
            round_b(0)
            act.wait_ge(s_wd, 1)
            act.activation(we[:, :], wd[:, :], ACT.Exp).then_inc(s_we, 1)
            act.wait_ge(s_cum, 1)

            def slot(g, t, e, odd, first):
                if first:
                    round_w(e, odd, 0)
                act.wait_ge(s_h0, g + 1)
                act.wait_ge(s_y0, g * 16 + DMA_CREDIT)
                act.activation(yo[:, 0:HALF], bank[0][:, :], ACT.Copy).then_inc(s_e0, 1)
                round_a(g + 1)
                round_b(g + 1)
                act.wait_ge(s_y1, g * 16 + DMA_CREDIT)
                act.activation(yo[:, HALF:H], bank[1][:, :], ACT.Copy).then_inc(s_e1, 1)
                if first:
                    round_w(e, odd, 1)

            slots(act, slot)

            def round_c(t):
                act.wait_ge(s_c1, (t + 1) * 2)
                act.wait_ge(s_m1, t)
                for h in range(2):
                    act.activation(l_hi[:, h * 4:(h + 1) * 4, :], c1[:, h * 4:(h + 1) * 4, :], ACT.Copy).then_inc(s_ch, 1)

            def root(t):
                act.wait_ge(s_ve, t + 1)
                act.activation(sd[:, :], ve[:, :], ACT.Sqrt).then_inc(s_sd, 1)

            round_c(0)
            root(0)
            with act.Fori(1, NT) as t:
                round_c(t)
                root(t)
            act.wait_ge(s_d2, 1)
            act.activation(we[:, :], wd[:, :], ACT.Exp).then_inc(s_ex2, 1)
            act.wait_ge(s_m0, NT)
            for h in range(2):
                act.activation(up_hi[:, h, :], lora_sb[:, h * HALF:(h + 1) * HALF], ACT.Copy).then_inc(s_uh, 1)
            for q in range(TQ):
                act.wait_ge(s_twt, q + 1)
                act.activation(twt_hi[:, q, :], bank[4 + q][:, :], ACT.Copy).then_inc(s_th, 1)

        @block.vector
        def _(dve):
            ch = Chain(dve, s_dve0)
            dve.wait_ge(s_mlp, 16)
            dve.wait_ge(s_pe0, 3)
            ch.link(dve.tensor_tensor(at_l[:, :], bank[6][0:B, 0:K8], c("b2", B), ALU.add))
            ch.link(dve.tensor_reduce(at_m[:, :], at_l[:, :], AX.X, ALU.max))
            dve.tensor_scalar(at_n[:, :], at_m[:, :], -1.0, None, ALU.mult).then_inc(s_sm, 1)
            dve.wait_ge(s_const, 16)
            dve.wait_ge(s_act0, 3)
            ch.link(dve.reciprocal(at_r[:, :], at_s[:, :]))
            ch.link(dve.tensor_scalar(att[:, :], at_e[:, :], at_r[:, 0:1], None, ALU.mult))
            dve.tensor_tensor(attx[:, :, :], c("ident", B)[:, 0:B].unsqueeze(2).to_broadcast([B, B, K8]),
                              att[:, :].unsqueeze(1).to_broadcast([B, B, K8]), ALU.mult).then_inc(s_attx, 1)
            dve.wait_ge(s_pe0, 5)
            ch.add(dve.tensor_copy(gsum[:, :], bank[2][:, 0:E]))
            ch.add(dve.tensor_copy(ctx0[:, :], bank[3][0:B, 0:CH]))
            dve.wait_ge(s_pe0, 6)
            spread = bank[5][:, 0:B * K8].rearrange("p (t q k) -> p t q k", q=2, k=K8)
            attp3 = attp[:, :].rearrange("p (t k) -> p t k", k=K8)
            for q in range(2):
                ch.add(dve.tensor_copy(attp3[q * CH:(q + 1) * CH, :, :], spread[q * CH:(q + 1) * CH, :, q, :]))
            ch.wait()
            ch.link(dve.tensor_tensor(aggb_t[:, :, :], attp3, c("kbias").unsqueeze(1).to_broadcast([P, NT, K8]), ALU.mult))
            ch.link(dve.tensor_reduce(aggb[:, :], aggb_t[:, :, :], AX.X, ALU.add))

            kern = c("kern").rearrange("p (k o) -> p k o", k=K8)

            def aggregate(ch, it, free):
                if free is not None:
                    for j in range(2):
                        dve.wait_ge(s_bd[j], free)
                w = attp[:, bass.ds(it * 2 * K8, 2 * K8)].rearrange("p (j k) -> p j k", j=2)
                ch.link(dve.tensor_tensor(prod, kern.unsqueeze(1).to_broadcast([P, 2, K8, CH]),
                                          w.unsqueeze(3).to_broadcast([P, 2, K8, CH]), ALU.mult))
                dve.tensor_reduce(agg[:, :, :], prod.rearrange("p j k o -> p j o k"), AX.X, ALU.add).then_inc(s_agg, 1)

            aggregate(ch, 0, None)

            oh4 = oh[:, :, :, :].rearrange("p j k e -> p (j k) e")
            rk4v = rk[:, :, :, :].rearrange("p j k e -> p (j k) e")
            iota4 = c("iota")[:, 0:E].unsqueeze(1).to_broadcast([P, 4, E])

            def take_rows(it):
                dve.wait_ge(s_g, it + 1)
                dve.tensor_copy(gt_sb[:, :], bank[4][0:E, 0:2 * P]).then_inc(s_gt, 1)

            def take_gate(it):
                dve.wait_ge(s_gg, it + 1)
                dve.tensor_copy(g_sb[:, :], bank[4][:, 2 * P:2 * P + 2 * E]).then_inc(s_gev, 1)

            def place(ch, it, nxt, first=False):
                dve.wait_ge(s_r, it + 1)
                ranks = bank[6][:, 0:2 * E].rearrange("p (j e) -> p j e", j=2)
                for k in range(2):
                    n = ch.add(dve.tensor_tensor(rk[:, :, k, :], oh[:, :, k, :], ranks, ALU.mult))
                ch.wait(n)
                ch.link(dve.tensor_reduce(rk4[:, :], rk4v, AX.X, ALU.add))
                ch.add(dve.tensor_copy(rank_all[:, bass.ds(it * 4, 4)], rk4[:, :]))
                ch.add(dve.tensor_copy(ix_all[:, bass.ds(it * 4, 4)], ixf[:, :]))
                ch.link(dve.scalar_tensor_tensor(pos_s[:, :], ixf[:, :], float(N), rk4[:, :], ALU.mult, ALU.add))
                ch.add(dve.tensor_scalar(lo_i[:, :], pos_s[:, :], P - 1, None, ALU.bitwise_and))
                ch.link(dve.tensor_scalar(hi_i[:, :], pos_s[:, :], P.bit_length() - 1, None, ALU.arith_shift_right))
                ch.add(dve.tensor_copy(lo_f[:, :], lo_i[:, :]))
                ch.link(dve.tensor_copy(hi_f[:, :], hi_i[:, :]))
                if nxt is not None:
                    take_gate(nxt)
                one_hot(it, first)

            def one_hot(it, first):
                if not first:
                    dve.wait_ge(s_list, it)
                for m in range(4):
                    dve.tensor_scalar(oh_lo[:, m, :], c("iota"), lo_f[:, m:m + 1], None, ALU.is_equal)
                    ins = dve.tensor_scalar(oh_hi[:, m, :], c("iota"), hi_f[:, m:m + 1],
                                            c("tok")[:, bass.ds(it * 2 + m // 2, 1)], ALU.is_equal, ALU.mult)
                ins.then_inc(s_hot, 1)

            def route(ch, it):
                dve.wait_ge(s_l, it + 1)
                for j in range(2):
                    n = ch.add(dve.scalar_tensor_tensor(lg[:, j, :], gsum[:, :], aggb[:, bass.ds(it * 2 + j, 1)],
                                                        bank[5][:, j * E:(j + 1) * E], ALU.mult, ALU.add))
                wait_apart(dve, s_chA, ch.base + n)
                for j in range(2):
                    n = ch.add(dve.max(mx[:, j, :], lg[:, j, :]))
                ch.wait(n)
                ch.add(dve.tensor_copy(mx_all[:, bass.ds(it * 2, 2), :], mx[:, :, 0:2]))
                for j in range(2):
                    ch.add(dve.max_index(ix[:, j, :], mx[:, j, :], lg[:, j, :]))
                ch.wait()
                ch.link(dve.tensor_copy(ixf[:, :].rearrange("p (j k) -> p j k", j=2), ix[:, :, 0:2]))
                ch.link(dve.tensor_tensor(oh4, iota4, ixf[:, :].unsqueeze(2).to_broadcast([P, 4, E]), ALU.is_equal))
                dve.wait_ge(s_m, it)
                ch.add(dve.tensor_copy(pre[:, 0, :], acc[:, :]))
                ch.link(dve.tensor_tensor(msk[:, :, :], oh[:, :, 0, :], oh[:, :, 1, :], ALU.add))
                ch.link(dve.tensor_tensor(pre[:, 1, :], pre[:, 0, :], msk[:, 0, :], ALU.add))
                dve.tensor_tensor(acc[:, :], pre[:, 1, :], msk[:, 1, :], ALU.add).then_inc(s_m, 1)

            LA = 23
            dve.wait_ge(s_init, 5)
            take_rows(0)
            take_gate(0)
            ca0 = Chain(dve, s_chA)
            route(ca0, 0)
            aggregate(ca0, 1, 2)
            take_rows(1)
            place(ca0, 0, 1, True)
            route(ca0, 1)
            aggregate(ca0, 2, 4)
            base = ca0.n
            with dve.Fori(2, NT // 2 - 1) as it:
                ch = Chain(dve, s_chA, (it - 2) * LA + base)
                take_rows(it)
                place(ch, it - 1, it)
                route(ch, it)
                aggregate(ch, it + 1, (it + 1) * 2)
                assert ch.n == LA, ch.n
            ch = Chain(dve, s_chA, base + LA * (NT // 2 - 3))
            it = NT // 2 - 1
            take_rows(it)
            place(ch, it - 1, it)
            route(ch, it)
            place(ch, it, None)
            dve.wait_ge(s_list, NT // 2)
            dve.tensor_copy(idx_all[:, :], bank[7][:, 0:P]).then_inc(s_ids, 1)

            ch = Chain(dve, s_chB)
            dve.wait_ge(s_cnt, 1)
            ch.link(dve.tensor_tensor(cmp[:, :, :], bank[4][:, 0:E].unsqueeze(2).to_broadcast([P, E, NT - 1]),
                                      c("thr").unsqueeze(1).to_broadcast([P, E, NT - 1]), ALU.is_gt))
            ch.link(dve.tensor_reduce(tl[:, :], cmp[:, :, :], AX.X, ALU.add))
            for e in range(E):
                ch.link(dve.scalar_tensor_tensor(cumf[:, e + 1:e + 2], tl[:, e:e + 1], 1.0, cumf[:, e:e + 1], ALU.add, ALU.add))
            ch.add(dve.tensor_scalar(cnt[:, 0:E], tl[:, :], 1.0, None, ALU.add))
            ch.link(dve.tensor_scalar(cnt[:, E:E + 1], cumf[:, E:E + 1], -1.0, float(SLOTS + 1), ALU.mult, ALU.add))
            dve.tensor_copy(cum[:, :], cumf[:, :]).then_inc(s_cum, 1)

            def rest_a(g):
                dve.wait_ge(s_ha, g + 1)
                dve.tensor_tensor(l_lo[:, 0:4, :], bank[2][:, :].rearrange("p (c m) -> p c m", c=4),
                                  l_hi[:, 0:4, :].bitcast(F32), ALU.subtract).then_inc(s_la, 1)

            def rest_b(g):
                dve.wait_ge(s_hb, g + 1)
                dve.tensor_tensor(l_lo[:, 4:8, :], bank[3][:, :].rearrange("p (c m) -> p c m", c=4),
                                  l_hi[:, 4:8, :].bitcast(F32), ALU.subtract).then_inc(s_lb, 1)

            rest_a(0)
            rest_b(0)
            dve.tensor_tensor(wd[:, :], mx_all[:, :, 1], mx_all[:, :, 0], ALU.subtract).then_inc(s_wd, 1)
            dve.wait_ge(s_we, 1)
            ch.link(dve.tensor_scalar(ws[:, :], we[:, :], 1.0, None, ALU.add))
            ch.link(dve.reciprocal(w_all[:, :, 0], ws[:, :]))
            ch.link(dve.tensor_tensor(w_all[:, :, 1], we[:, :], w_all[:, :, 0], ALU.mult))
            ch.link(dve.tensor_tensor(sel[:, :, :], c("iota")[:, 0:E].unsqueeze(1).to_broadcast([P, 2 * NT, E]),
                                      ix_all[:, :].unsqueeze(2).to_broadcast([P, 2 * NT, E]), ALU.is_equal))
            ch.link(dve.tensor_tensor(sel[:, :, :], sel[:, :, :],
                                      cumf[:, 0:E].unsqueeze(1).to_broadcast([P, 2 * NT, E]), ALU.mult))
            ch.link(dve.tensor_reduce(base_f[:, :], sel[:, :, :], AX.X, ALU.add))
            dve.scalar_tensor_tensor(pos_all[:, :], base_f[:, :], float(P), rank_all[:, :], ALU.mult, ALU.add).then_inc(s_pall, 1)

            def rest_w(e, odd, half):
                for k in range(HC // 2):
                    at = half * (HC // 2) + k
                    dve.wait_ge(s_hi, e * HC + (HC + at + 1))
                    dve.tensor_tensor(w_lo[1 - odd][:, at, :], raw[k], w_hi[1 - odd][:, at, :].bitcast(F32),
                                      ALU.subtract).then_inc(s_lo, 1)

            def slot(g, t, e, odd, first):
                if first:
                    rest_w(e, odd, 0)
                rest_a(g + 1)
                rest_b(g + 1)
                if first:
                    rest_w(e, odd, 1)

            dve.wait_ge(s_lo, HC)
            slots(dve, slot)

            dve.wait_ge(s_late, 64)
            dve.wait_ge(s_xr[0], 16)
            dve.tensor_tensor(ctxx, c("ident", B)[:, 0:B].unsqueeze(2).to_broadcast([B, B, CH]),
                              ctx0[:, :].unsqueeze(1).to_broadcast([B, B, CH]), ALU.mult).then_inc(s_cxx, 1)

            def take_context():
                dve.wait_ge(s_cxb, 1)
                ctx4 = ctxb[:, :, :].rearrange("p (q n) o -> p q n o", q=4)
                for q in range(4):
                    dve.tensor_tensor(ctx4[:, q], bank[CTX_BANKS[q]][:, :].rearrange("p (n o) -> p n o", o=CH),
                                      c("fside").unsqueeze(1).to_broadcast([P, B // 4, CH]), ALU.add).then_inc(s_cx, 1)
                dve.wait_ge(s_cx, 4)

            LC = 15
            def combine(ch, t, j, it):
                dve.wait_ge(s_yg[j][0], (it + 1) * 16)
                dve.wait_ge(s_xr[j], (it + 1) * 16)
                rows = res[:, bass.ds(t, 1), :].rearrange("p o n -> p (o n)")
                w2 = w_all[:, bass.ds(t, 1), :].rearrange("p o k -> p (o k)")
                ch.link(dve.scalar_tensor_tensor(rows, yg[j][:, 0, :], w2[:, 0:1], rows, ALU.mult, ALU.add))
                wait_apart(dve, s_yg[j][1], (it + 1) * 16)
                dve.scalar_tensor_tensor(rows, yg[j][:, 1, :], w2[:, 1:2], rows, ALU.mult, ALU.add).then_inc(s_x1, 1)

            def take_conv(t):
                out4 = c1.rearrange("p k (b u o) -> p b u k o", b=2, u=CQ)
                for b in range(2):
                    dve.wait_ge(s_cv, t * 2 + b + 1)
                    if b == 0 and not isinstance(t, int):
                        dve.wait_ge(s_cl, t * 2)
                    add = ctxb[:, bass.ds(t * 2 + b, 1), :].rearrange("p n (u o) -> p (n u) o", u=CQ)
                    ps = bank[4 + b][:, :].rearrange("p (u k o) -> p u k o", u=CQ, k=HC)
                    dve.tensor_tensor(out4[:, b], ps, add.unsqueeze(2).to_broadcast([P, CQ, HC, CP]), ALU.add).then_inc(s_c1, 1)

            def rest_c(t):
                for h in range(2):
                    dve.wait_ge(s_ch, t * 2 + h + 1)
                    dve.tensor_tensor(l_lo[:, h * 4:(h + 1) * 4, :], c1[:, h * 4:(h + 1) * 4, :],
                                      l_hi[:, h * 4:(h + 1) * 4, :].bitcast(F32), ALU.subtract).then_inc(s_cl, 1)

            def gate(ch, t):
                dve.wait_ge(s_g1, t + 1)
                down = down_all[:, bass.ds(t, 1), :].rearrange("p o n -> p (o n)")
                dve.tensor_copy(down, bank[2][:, 0:E * R])
                dve.tensor_tensor(hb[:, :], bank[2][:, E * R:G1W], d("gb1"), ALU.add).then_inc(s_g1e, 1)
                wait_apart(dve, s_g1e, t + 1 + CREDIT)
                ch.add(dve.bn_stats(st[:, :], hb[:, :]))
                wait_apart(dve, s_chC, ch.base + ch.n)
                ch.link(dve.bn_aggr(mv[:, :], st[:, :]))
                dve.tensor_scalar(ve[:, :], mv[:, 1:2], LN_EPS, None, ALU.add).then_inc(s_ve, 1)
                dve.wait_ge(s_sd, t + 1)
                ch.link(dve.reciprocal(rs[:, :], sd[:, :]))
                ch.link(dve.tensor_scalar(hn[:, :], hb[:, :], mv[:, 0:1], rs[:, 0:1], ALU.subtract, ALU.mult))
                ch.link(dve.tensor_tensor(hb[:, :], hn[:, :], d("gamma"), ALU.mult))
                ch.link(dve.tensor_tensor(hn[:, :], hb[:, :], d("beta"), ALU.add))
                ch.link(dve.scalar_tensor_tensor(hp[:, :, :], hn[:, :].unsqueeze(1).to_broadcast([P, E, HG]), 0.0,
                                                 d("gw2").rearrange("p (e h) -> p e h", e=E), ALU.max, ALU.mult))
                ch.link(dve.tensor_reduce(gl[:, :], hp[:, :, :], AX.X, ALU.add))
                ch.add(dve.tensor_tensor(gt[:, :], gl[:, :], d("gb2"), ALU.add))
                wait_apart(dve, s_chC, ch.base + ch.n)
                ch.link(dve.max(mx2[:, :], gt[:, :]))
                ch.add(dve.tensor_copy(mx2_all[:, bass.ds(t, 1), :].rearrange("p o k -> p (o k)"), mx2[:, 0:2]))
                ch.link(dve.max_index(ix2[:, :], mx2[:, :], gt[:, :]))
                ch.link(dve.tensor_copy(ixf2[:, :], ix2[:, 0:2]))
                ohv = oh_all[:, bass.ds(t, 1), :, :].rearrange("p o k e -> p (o k) e")
                ch.link(dve.tensor_tensor(ohv, c("iota")[:, 0:E].unsqueeze(1).to_broadcast([P, 2, E]),
                                          ixf2[:, :].unsqueeze(2).to_broadcast([P, 2, E]), ALU.is_equal))
                acc2v = acc2[:, :].rearrange("p (k e) -> p k e", k=2)
                dve.wait_ge(s_a2, t + CREDIT)
                dve.tensor_tensor(acc2v, acc2v, ohv, ALU.add).then_inc(s_a2, 1)

            def take_main(t):
                rows = res[:, bass.ds(t, 1), :].rearrange("p o n -> p (o n)")
                for h, (s, done) in enumerate(((s_m0, s_me0), (s_m1, s_me1))):
                    dve.wait_ge(s, t + 1)
                    half = rows[:, h * HALF:(h + 1) * HALF]
                    dve.tensor_tensor(half, bank[h][:, :], half, ALU.add).then_inc(done, 1)

            ch = Chain(dve, s_chC)
            combine(ch, 0, 0, 0)
            combine(ch, 1, 1, 0)
            take_context()
            take_conv(0)
            with dve.Fori(0, NT // 2 - 1) as i:
                ch = Chain(dve, s_chC, i * (2 * LC) + 2)
                for j in range(2):
                    t = i * 2 + j
                    rest_c(t)
                    combine(ch, t + 2, j, i + 1)
                    gate(ch, t)
                    take_conv(t + 1)
                    take_main(t)
                assert ch.n == 2 * LC, ch.n
            ch = Chain(dve, s_chC, (NT // 2 - 1) * 2 * LC + 2)
            rest_c(NT - 2)
            gate(ch, NT - 2)
            take_conv(NT - 1)
            take_main(NT - 2)
            rest_c(NT - 1)
            gate(ch, NT - 1)

            ch = Chain(dve, s_chD)
            dve.tensor_tensor(wd[:, :], mx2_all[:, :, 1], mx2_all[:, :, 0], ALU.subtract).then_inc(s_d2, 1)
            dve.wait_ge(s_ex2, 1)
            ch.link(dve.tensor_scalar(ws[:, :], we[:, :], 1.0, None, ALU.add))
            ch.link(dve.reciprocal(g2[:, :, 0], ws[:, :]))
            ch.link(dve.tensor_tensor(g2[:, :, 1], we[:, :], g2[:, :, 0], ALU.mult))
            dve.wait_ge(s_t2, 1)
            ch.link(dve.tensor_scalar(allow[:, :], bank[2][:, 0:2 * E], float(CAPACITY), None, ALU.is_le))
            oh_t = oh_all[:, :, :, :].rearrange("p t k e -> p t (k e)")
            oh_k = oh_all[:, :, :, :].rearrange("p t k e -> p (t k) e")
            ch.link(dve.tensor_tensor(oh_t, oh_t, allow[:, :].unsqueeze(1).to_broadcast([P, NT, 2 * E]), ALU.mult))
            g2v = g2[:, :, :].rearrange("p t k -> p (t k)").unsqueeze(2).to_broadcast([P, 2 * NT, E])
            ch.link(dve.tensor_tensor(oh_k, oh_k, g2v, ALU.mult))
            ch.link(dve.tensor_tensor(w2_all[:, :, :], oh_all[:, :, 0, :], oh_all[:, :, 1, :], ALU.add))

            for q in range(TQ):
                rows = down_all[:, q * TG:(q + 1) * TG, :].rearrange("p t (e r) -> p (t e) r", r=R)
                w = w2_all[:, q * TG:(q + 1) * TG, :].rearrange("p t e -> p (t e)").unsqueeze(2).to_broadcast([P, TG * E, R])
                dve.scalar_tensor_tensor(rows, rows, ALPHA, w, ALU.mult, ALU.mult).then_inc(s_tw, 1)
            for h in range(2):
                dve.wait_ge(s_uh, h + 1)
                dve.tensor_tensor(up_lo[:, h, :], lora_sb[:, h * HALF:(h + 1) * HALF], up_hi[:, h, :].bitcast(F32),
                                  ALU.subtract).then_inc(s_ul, 1)
            take_main(NT - 1)
            for q in range(TQ):
                dve.wait_ge(s_th, q + 1)
                dve.tensor_tensor(twt_lo[:, q, :], bank[4 + q][:, :], twt_hi[:, q, :].bitcast(F32),
                                  ALU.subtract).then_inc(s_tl, 1)
            with dve.Fori(0, NT // RING) as i:
                for j in range(RING):
                    t = i * RING + j
                    rows = res[:, bass.ds(t, 1), :].rearrange("p o (q w) -> p (o w) q", q=PH)
                    to = ring[j].rearrange("p (w q) -> p w q", q=PH)
                    dve.wait_ge(s_out[j], i * 16 + DMA_CREDIT)
                    for h in range(2):
                        dve.wait_ge(s_up, t * 2 + h + 1)
                        w = slice(h * P // 2, (h + 1) * P // 2)
                        dve.tensor_tensor(to[:, w, :], bank[2 * (1 - j % 2) + h][:, :].rearrange("p (w q) -> p w q", q=PH),
                                          rows[:, w, :], ALU.add).then_inc(s_fin, 1)

        @block.tensor
        def _(pe):
            ones = c("ones")
            ident = c("ident")
            gatec = c("gate").rearrange("p (c e) -> p c e", c=HC)
            pe.wait_ge(s_mlp, 16)
            pe.matmul(bank[0][:, 0:B], c("w0"), c("emb"), start=True, stop=True).then_inc(s_pe0, 1)

            def gate_products(it, i, p, first):
                if not first:
                    pe.wait_ge(s_gev, it)
                for j in range(2):
                    pe.wait_ge(s_xt[p][j], (i + 1) * 16)
                for k in range(HC):
                    mm = pe.matmul(bank[4][0:E, 0:2 * P], gatec[:, k, :], xt_pair[p][:, k], start=(k == 0), stop=(k == HC - 1))
                mm.then_inc(s_g, 1)

            def turn_gate(it):
                wait_apart(pe, s_gt, it + 1)
                for j in range(2):
                    mm = pe.transpose(bank[4][:, 2 * P + j * E:2 * P + (j + 1) * E], gt_sb[:, j * P:(j + 1) * P],
                                      c("ident", E)[:, 0:E])
                mm.then_inc(s_gg, 1)

            pe.wait_ge(s_act0, 1)
            pe.matmul(bank[1][:, 0:B], c("w1"), h0[:, :], start=True, stop=True).then_inc(s_pe0, 1)
            pe.wait_ge(s_act0, 2)
            pe.matmul(bank[6][0:B, 0:K8], h1[:, :], c("w2"), start=True, stop=True).then_inc(s_pe0, 1)
            pe.wait_ge(s_const, 16)
            for k in range(HC):
                mm = pe.matmul(bank[2][:, 0:E], ones, gatec[:, k, :], start=(k == 0), stop=(k == HC - 1))
            mm.then_inc(s_pe0, 1)
            pe.matmul(bank[3][0:B, 0:CH], c("emb"), c("cw"), start=True, stop=True).then_inc(s_pe0, 1)
            pe.wait_ge(s_attx, 1)
            pe.matmul(bank[5][:, 0:B * K8], c("ones", B), attx[:, :, :].rearrange("p n k -> p (n k)"),
                      start=True, stop=True).then_inc(s_pe0, 1)
            gate_products(0, 0, 0, True)
            pe.wait_ge(s_agg, 1)

            def ranks(it):
                pe.wait_ge(s_m, it + 1)
                pe.matmul(bank[6][:, 0:2 * E], c("tri"), msk[:, :, :].rearrange("p j e -> p (j e)"), start=True, stop=False)
                pe.matmul(bank[6][:, 0:2 * E], ones, pre[:, :, :].rearrange("p j e -> p (j e)"),
                          start=False, stop=True).then_inc(s_r, 1)

            def lists(it, first, last):
                pe.wait_ge(s_hot, it + 1)
                for m in range(4):
                    mm = pe.matmul(bank[7][:, 0:P], oh_lo[:, m, :], oh_hi[:, m, :], start=(first and m == 0), stop=(last and m == 3))
                mm.then_inc(s_list, 1)

            def phase_a(it, i, p, first=False, second=False):
                if not first:
                    gate_products(it, i, p, False)
                    ranks(it - 1)
                for j in range(2):
                    if not first:
                        pe.wait_ge(s_cev[j], it * 2)
                    pe.wait_ge(s_bd[j], (it + 1) * 2)
                    pe.wait_ge(s_x[p][j], (i + 1) * 16)
                    for h in range(2):
                        mm = pe.matmul(bank[2 * j + h][:, :], bd[j][:, :], x_sb[p][j][:, h * HALF:(h + 1) * HALF], start=True, stop=True)
                    mm.then_inc(s_c[j], 1)
                    if j == 0:
                        turn_gate(it)
                pe.wait_ge(s_gev, it + 1)
                for j in range(2):
                    mm = pe.matmul(bank[5][:, j * E:(j + 1) * E], bd[j][:, :], g_sb[:, j * E:(j + 1) * E], start=True, stop=True)
                mm.then_inc(s_l, 1)
                if not first:
                    lists(it - 1, second, False)

            phase_a(0, 0, 0, first=True)
            phase_a(1, 0, 1, second=True)
            with pe.Fori(1, NT // 4) as i:
                for p in range(2):
                    phase_a(i * 2 + p, i, p)
            ranks(NT // 2 - 1)
            lists(NT // 2 - 1, False, True)
            pe.wait_ge(s_gev, NT // 2)
            pe.matmul(bank[4][:, 0:E], ones, acc[:, :], start=True, stop=True).then_inc(s_cnt, 1)
            for j in range(2):
                pe.wait_ge(s_cev[j], NT)

            def transposes(g):
                pe.wait_ge(s_xg, (g + 1) * 16)
                for half, (bk, s) in enumerate(((2, s_ta), (3, s_tb))):
                    for k in range(4):
                        at = half * 4 + k
                        mm = pe.transpose(bank[bk][:, k * P:(k + 1) * P], xg[:, at * P:(at + 1) * P], ident)
                    mm.then_inc(s, 1)

            transposes(0)
            pe.wait_ge(s_cum, 1)

            def product(k, to, wh, wl, cols):
                for n, (a, b) in enumerate(((l_lo, wh), (l_hi, wh), (l_hi, wl))):
                    mm = pe.matmul(to[:, :], a[:, k, :], b[:, k, cols * HALF:(cols + 1) * HALF],
                                   start=(k == 0 and n == 0), stop=(k == HC - 1 and n == 2))
                return mm

            def slot(g, t, e, odd, first):
                if first:
                    pe.wait_ge(s_lo, (e + 1) * HC)
                pe.wait_ge(s_e0, g + CREDIT)
                pe.wait_ge(s_la, g + 1)
                for k in range(HC):
                    if k == 4:
                        pe.wait_ge(s_lb, g + 1)
                    mm = product(k, bank[0], w_hi[odd], w_lo[odd], 0)
                mm.then_inc(s_h0, 1)
                transposes(g + 1)
                pe.wait_ge(s_e1, g + CREDIT)
                for k in range(HC):
                    mm = product(k, bank[1], w_hi[odd], w_lo[odd], 1)
                    if k == 3:
                        mm.then_inc(s_fa, 1)
                mm.then_inc(s_h1, 1)

            slots(pe, slot)

            total = pe.value_load(cum[0:1, E:E + 1], min_val=E, max_val=SLOTS)
            pe.wait_ge(s_late, 64)
            pe.wait_ge(s_e0, total + CREDIT)
            pe.wait_ge(s_e1, total + CREDIT)
            wait_apart(pe, s_lb, total + 1)
            pe.wait_ge(s_cxx, 1)
            for q in range(4):
                mm = pe.matmul(bank[CTX_BANKS[q]][:, :], c("ones", B),
                               ctxx[:, q * 8:(q + 1) * 8, :].rearrange("p n o -> p (n o)"), start=True, stop=True)
            mm.then_inc(s_cxb, 1)

            def conv(t, rel, free):
                pe.wait_ge(s_rel, rel)
                if free is not None:
                    pe.wait_ge(s_c1, free)
                for b in range(2):
                    for u in range(CQ):
                        for m in range(MC):
                            at = (u * MC + m) * P
                            for k in range(WINS):
                                mm = pe.matmul(bank[4 + b][:, at:at + P], x1p[:, b, u, m * P + k:(m + 1) * P + k],
                                               conv_sb[:, k, u, :], start=(k == 0), stop=(k == WINS - 1))
                    mm.then_inc(s_cv, 1)

            def down(t):
                pe.wait_ge(s_c1, (t + 1) * 2)
                pe.wait_ge(s_g1e, t + CREDIT)
                for k in range(HC):
                    mm = pe.matmul(bank[2][:, 0:G1W], c1[:, k, :], down_sb[:, k, :], start=(k == 0), stop=(k == HC - 1))
                mm.then_inc(s_g1, 1)

            def main(t, last=False):
                for h, (s, done) in enumerate(((s_m0, s_me0), (s_m1, s_me1))):
                    if last and h == 1:
                        pe.wait_ge(s_a2, NT + CREDIT)
                        pe.matmul(bank[2][:, 0:2 * E], ones, acc2[:, :], start=True, stop=True).then_inc(s_t2, 1)
                    pe.wait_ge(done, t + CREDIT)
                    for k in range(HC):
                        if h == 0 and k % 4 == 0:
                            pe.wait_ge(s_cl, t * 2 + k // 4 + 1)
                        mm = product(k, bank[h], w_hi[0], w_lo[0], h)
                    mm.then_inc(s, 1)

            pe.wait_ge(s_pad, 2)
            conv(0, PH * 16, None)
            pe.wait_ge(s_cx, 4)
            with pe.Fori(0, NT - 1) as t:
                down(t)
                conv(t + 1, (t + 2) * (PH * 16), (t + 1) * 2)
                main(t)
            down(NT - 1)
            main(NT - 1, True)

            for q in range(TQ):
                pe.wait_ge(s_tw, q + 1)
                for t in range(q * TG, (q + 1) * TG):
                    mm = pe.transpose(bank[4 + q][:, (t % TG) * P:(t % TG + 1) * P], down_all[:, t, :], ident)
                mm.then_inc(s_twt, 1)
            pe.wait_ge(s_ul, 2)
            for t in range(NT):
                q, at = t // TG, (t % TG) * P
                if t % TG == 0:
                    pe.wait_ge(s_tl, q + 1)
                if t == 1:
                    pe.wait_ge(s_me1, NT + CREDIT)
                if t >= 2:
                    pe.wait_ge(s_fin, (t - 1) * 2)
                for h in range(2):
                    for n, (a, b) in enumerate(((twt_lo, up_hi), (twt_hi, up_hi), (twt_hi, up_lo))):
                        mm = pe.matmul(bank[2 * (1 - t % 2) + h][:, :], a[:, q, at:at + P], b[:, h, :], start=(n == 0), stop=(n == 2))
                    mm.then_inc(s_up, 1)


INPUTS = ["x", "x_t", "x_ph", "consts_a", "consts_b", "expert_w", "conv_w", "down_w", "lora_b"]


def lay_out(i):
    f = np.float32
    a = np.zeros((P, CA_W), f)
    b = np.zeros((P, CB_W), f)

    def put(to, where, name, v):
        lo, hi = where[name]
        to[:, lo:hi] = np.reshape(v, (-1, hi - lo)) if np.ndim(v) else v

    put(a, CA, "emb", i["cond_128"].T)
    put(a, CA, "w0", i["L0_cond_W0"])
    put(a, CA, "w1", i["L0_cond_W1"])
    put(a, CA, "w2", i["L0_cond_W2"])
    put(a, CA, "b0", i["L0_cond_b0"][:, None])
    put(a, CA, "b1", i["L0_cond_b1"][:, None])
    put(a, CA, "b2", np.broadcast_to(i["L0_cond_b2"], (P, K8)))
    put(a, CA, "gate", i["L0_ffn_gate_w"].reshape(HC, P, E).transpose(1, 0, 2).reshape(P, -1))
    kern = i["L0_cond_weight"][..., 0].transpose(2, 0, 1).reshape(CH, -1)
    put(a, CA, "kern", np.concatenate([kern, kern]))
    put(a, CA, "kbias", np.concatenate([i["L0_cond_bias_k"].T] * 2))
    put(a, CA, "ident", np.eye(P, dtype=f))
    put(a, CA, "tri", np.triu(np.ones((P, P), f), 1))
    put(a, CA, "ones", np.ones((P, P), f))
    put(a, CA, "iota", np.broadcast_to(np.arange(P, dtype=f), (P, P)))
    put(a, CA, "thr", np.broadcast_to(np.arange(1, NT, dtype=f) * P, (P, NT - 1)))
    put(a, CA, "cw", i["L1_cond_c_weight"].T)
    put(a, CA, "fside", np.broadcast_to(i["fside_S_0"], (P, CH)))
    put(a, CA, "tok", np.arange(NT, dtype=f)[None, :] * P + np.arange(P, dtype=f)[:, None])
    put(b, CB, "gb1", np.broadcast_to(i["L1_ffn_gb1"], (P, HG)))
    put(b, CB, "gamma", np.broadcast_to(i["L1_ffn_ln_gamma"], (P, HG)))
    put(b, CB, "beta", np.broadcast_to(i["L1_ffn_ln_beta"], (P, HG)))
    put(b, CB, "gb2", np.broadcast_to(i["L1_ffn_gb2"], (P, E)))
    put(b, CB, "gw2", np.broadcast_to(i["L1_ffn_gw2"].reshape(-1), (P, E * HG)))

    w = i["L1_cond_weight"]
    per = w.shape[1]
    conv = np.zeros((PH, CP, WINS, CQ, PH, CP), f)
    for qi in range(PH):
        for qo in range(PH):
            for k in range(WINS):
                tap = PH * k + (qi + PAD) % PH - qo
                if 0 <= tap < TAPS:
                    for g in range(CH // per):
                        u, at = divmod(g * per, CP)
                        s = slice(at, at + per)
                        conv[qi, s, k, u, qo, s] = w[g * per:(g + 1) * per, :, tap].T

    def to_phases(m):
        return np.ascontiguousarray(m.reshape(*m.shape[:-1], P, PH).swapaxes(-1, -2)).reshape(m.shape)

    def by_phase(m):
        return m.reshape(MC, P, PH, -1).transpose(1, 0, 2, 3).reshape(P, HC, -1)

    down = np.concatenate([by_phase(i["L1_ffn_lora_A"].transpose(1, 0, 2).reshape(H, E * R)),
                           by_phase(i["L1_ffn_gw1"].T)], axis=2)
    x = i["x"].reshape(N, H)
    return {
        "x": x,
        "x_t": x.reshape(NT, P, HC, P).transpose(0, 3, 2, 1).reshape(NT * P, H),
        "consts_a": a,
        "consts_b": b,
        "x_ph": to_phases(x),
        "expert_w": to_phases(np.concatenate([i["L0_ffn_expert_w"].reshape(E, HC, P, H),
                                              by_phase(i["L1_ffn_weight"].T).transpose(1, 0, 2)[None]])),
        "conv_w": conv.reshape(P, WINS, CQ, P),
        "down_w": down,
        "lora_b": i["L1_ffn_lora_B"].reshape(E * R, H),
    }


def kernel(**inputs):
    import concourse.bacc as bacc
    from concourse.bass_utils import run_bass_kernel_spmd

    nc = bacc.Bacc("TRN2", target_bir_lowering=False, num_devices=1)
    laid = lay_out({k: np.asarray(v) for k, v in inputs.items()})
    arrays, args = {}, []
    for name in INPUTS:
        a = np.ascontiguousarray(laid[name])
        arrays[f"in_{name}"] = a
        args.append(nc.dram_tensor(f"in_{name}", a.shape, mybir.dt.from_np(a.dtype), kind="ExternalInput").ap())
    out = nc.dram_tensor("out_0", (N, H), F32, kind="ExternalOutput").ap()
    build(nc, *args, out)
    r = run_bass_kernel_spmd(nc, [arrays], core_ids=[0])
    return r.results[0]["out_0"].reshape(B, CH, H)
```
